# Optimizing a Trainium2 kernel written in Bass

```python
import numpy as np
import jax
import jax.numpy as jnp

def _softmax(x, axis=-1):
    return jax.nn.softmax(x, axis=axis)

def _gelu(x):
    return jax.nn.gelu(x, approximate=True)

def _silu(x):
    return jax.nn.silu(x)

def _sigmoid(x):
    return jax.nn.sigmoid(x)

def _layernorm(x, axis=-1, eps=1e-05):
    m = jnp.mean(x, axis=axis, keepdims=True)
    v = jnp.var(x, axis=axis, keepdims=True)
    return (x - m) / jnp.sqrt(v + eps)

def _scatter_add(tgt, idx, src, axis=0):
    return tgt.at[idx].add(src)

def _segment_sum(src, seg, n):
    return jax.ops.segment_sum(src, seg, n)
kernel_name = 'mk_adj_resnorm_d1_adj_r2_423bc6'

def setup_inputs(seed: int=0):
    np.random.seed(seed)
    _w = jnp.asarray

    def _rec_inputs():
        import jax
        import jax.numpy as jnp
        _gk = jax.random.key(seed)
        x = -0.0001538 + 1 * jax.random.normal(jax.random.fold_in(_gk, 1), (16, 512, 384), jnp.float32)
        _a = jax.random.bernoulli(jax.random.fold_in(_gk, 2), 0.0078125, (16, 512, 512))
        _a = jnp.logical_or(_a, jnp.swapaxes(_a, -1, -2))
        _a = jnp.logical_or(_a, jnp.eye(512, dtype=bool))
        _af = _a.astype(jnp.float32)
        _af = _af * jax.random.uniform(jax.random.fold_in(_gk, 3), (16, 512, 512), jnp.float32, 0.05, 5.06092)
        adj = _af
        return (x, adj)
    x, adj = _rec_inputs()

    def _L0_gnn_setup():
        import jax, jax.numpy as jnp
        import numpy as np
        D_MODEL = 384
        NHEADS = 8
        D_FF = 1536
        B, N = (8, 512)
        EPS = 1e-06

        def _rmsnorm(x, alpha, gamma):
            x = x * jax.lax.rsqrt(jnp.mean(x * x, axis=-1, keepdims=True) + EPS)
            return alpha * x + gamma
        key = jax.random.key(seed)
        ks = jax.random.split(key, 10)
        d, f = (D_MODEL, D_FF)
        s = 1.0 / np.sqrt(d)
        inp = {'x': jax.random.normal(ks[0], (B, N, d), dtype=jnp.float32), 'attn_bias': jax.random.normal(ks[1], (B, N, N), dtype=jnp.float32), 'wq': jax.random.normal(ks[2], (d, d), dtype=jnp.float32) * s, 'bq': jnp.zeros((d,), jnp.float32), 'wk': jax.random.normal(ks[3], (d, d), dtype=jnp.float32) * s, 'bk': jnp.zeros((d,), jnp.float32), 'wv': jax.random.normal(ks[4], (d, d), dtype=jnp.float32) * s, 'bv': jnp.zeros((d,), jnp.float32), 'wo': jax.random.normal(ks[5], (d, d), dtype=jnp.float32) * s, 'bo': jnp.zeros((d,), jnp.float32), 'w1': jax.random.normal(ks[6], (d, f), dtype=jnp.float32) * s, 'b1': jnp.zeros((f,), jnp.float32), 'w2': jax.random.normal(ks[7], (f, d), dtype=jnp.float32) * (1.0 / np.sqrt(f)), 'b2': jnp.zeros((d,), jnp.float32), 'alpha1': jnp.ones((d,), jnp.float32), 'gamma1': jnp.ones((d,), jnp.float32), 'alpha2': jnp.ones((d,), jnp.float32), 'gamma2': jnp.ones((d,), jnp.float32)}
        return inp
    _L0_gnn_all = _L0_gnn_setup()
    _L0_gnn_in = {k: v for k, v in _L0_gnn_all.items() if k in ('wq', 'bq', 'wk', 'bk', 'wv', 'bv', 'wo', 'bo', 'w1', 'b1', 'w2', 'b2', 'alpha1', 'gamma1', 'alpha2', 'gamma2')}
    del _L0_gnn_all
    return {'x': x, 'adj': adj, 'L0_gnn_wq': _L0_gnn_in['wq'], 'L0_gnn_bq': _L0_gnn_in['bq'], 'L0_gnn_wk': _L0_gnn_in['wk'], 'L0_gnn_bk': _L0_gnn_in['bk'], 'L0_gnn_wv': _L0_gnn_in['wv'], 'L0_gnn_bv': _L0_gnn_in['bv'], 'L0_gnn_wo': _L0_gnn_in['wo'], 'L0_gnn_bo': _L0_gnn_in['bo'], 'L0_gnn_w1': _L0_gnn_in['w1'], 'L0_gnn_b1': _L0_gnn_in['b1'], 'L0_gnn_w2': _L0_gnn_in['w2'], 'L0_gnn_b2': _L0_gnn_in['b2'], 'L0_gnn_alpha1': _L0_gnn_in['alpha1'], 'L0_gnn_gamma1': _L0_gnn_in['gamma1'], 'L0_gnn_alpha2': _L0_gnn_in['alpha2'], 'L0_gnn_gamma2': _L0_gnn_in['gamma2']}

def reference(x, adj, L0_gnn_wq, L0_gnn_bq, L0_gnn_wk, L0_gnn_bk, L0_gnn_wv, L0_gnn_bv, L0_gnn_wo, L0_gnn_bo, L0_gnn_w1, L0_gnn_b1, L0_gnn_w2, L0_gnn_b2, L0_gnn_alpha1, L0_gnn_gamma1, L0_gnn_alpha2, L0_gnn_gamma2):
    import jax
    import jax.numpy as jnp

    def _L0_gnn_ref(x, attn_bias, wq, bq, wk, bk, wv, bv, wo, bo, w1, b1, w2, b2, alpha1, gamma1, alpha2, gamma2):
        import jax, jax.numpy as jnp
        import numpy as np
        D_MODEL = 384
        NHEADS = 8
        D_FF = 1536
        B, N = (8, 512)
        EPS = 1e-06

        def _rmsnorm(x, alpha, gamma):
            x = x * jax.lax.rsqrt(jnp.mean(x * x, axis=-1, keepdims=True) + EPS)
            return alpha * x + gamma
        b, n, d = x.shape
        h = NHEADS
        dh = d // h
        scaling = dh ** (-0.5)

        def split_heads(t):
            return t.reshape(b, n, h, dh).transpose(0, 2, 1, 3)
        q = split_heads(x @ wq + bq)
        k = split_heads(x @ wk + bk)
        v = split_heads(x @ wv + bv)
        scores = jnp.einsum('bhqd,bhkd->bhqk', q, k) * scaling
        scores = scores + attn_bias[:, None, :, :]
        attn = jax.nn.softmax(scores, axis=-1)
        ctx = jnp.einsum('bhij,bhjd->bhid', attn, v)
        ctx = ctx.transpose(0, 2, 1, 3).reshape(b, n, d)
        attn_out = ctx @ wo + bo
        x = _rmsnorm(x + attn_out, alpha1, gamma1)
        ff = jax.nn.silu(x @ w1 + b1) @ w2 + b2
        x = _rmsnorm(x + ff, alpha2, gamma2)
        return x
    x = _layernorm(x + _L0_gnn_ref(x, adj, L0_gnn_wq, L0_gnn_bq, L0_gnn_wk, L0_gnn_bk, L0_gnn_wv, L0_gnn_bv, L0_gnn_wo, L0_gnn_bo, L0_gnn_w1, L0_gnn_b1, L0_gnn_w2, L0_gnn_b2, L0_gnn_alpha1, L0_gnn_gamma1, L0_gnn_alpha2, L0_gnn_gamma2), axis=-1)
    return x

_drawn_inputs = setup_inputs


def setup_inputs(seed=0):
    import zlib

    import numpy as np

    out = dict(_drawn_inputs(seed))
    spreads = {'L0_gnn_bq': (0.0, 0.8),
     'L0_gnn_bk': (0.0, 0.8),
     'L0_gnn_bv': (0.0, 0.1),
     'L0_gnn_bo': (0.0, 0.1),
     'L0_gnn_b1': (0.0, 0.34),
     'L0_gnn_b2': (0.0, 0.1),
     'L0_gnn_alpha1': (1.0, 0.2),
     'L0_gnn_gamma1': (1.0, 0.2),
     'L0_gnn_alpha2': (1.0, 0.2),
     'L0_gnn_gamma2': (1.0, 0.2)}
    factors = {}
    for name, (base, spread) in spreads.items():
        noise = np.random.default_rng([zlib.crc32(name.encode()), seed]).standard_normal(out[name].shape)
        drawn = base * np.exp(spread * noise) if base else spread * noise
        out[name] = jnp.asarray(drawn.astype(out[name].dtype))
    for name, factor in factors.items():
        out[name] = (out[name] * factor).astype(out[name].dtype)
    return out
```

```python
from contextlib import ExitStack

import concourse.bass as bass
from concourse import mybir

FP32 = mybir.dt.float32
FP32R = mybir.dt.float32r
ALU = mybir.AluOpType
ACT = mybir.ActivationFunctionType

P = 128
B, N, D = 16, 512, 384
H = 8
DH = D // H
F = 1536
TT = N // P
KT = D // P
JT = F // P
LAST = B - 1
EPS_RMS = 1e-6
EPS_LN = 1e-5
BIG = 3.0e38
DMA = 16


def pieces_of_head(h):
    out, f, end = [], h * DH, (h + 1) * DH
    while f < end:
        t = f // P
        n = min(end, (t + 1) * P) - f
        out.append((t, f - t * P, f - h * DH, n))
        f += n
    return out


def heads_of_tile(t):
    return [h for h in range(H) if any(p[0] == t for p in pieces_of_head(h))]


LO = 64
V_COLS = LO + DH

Q_DMAS = [4 * len(heads_of_tile(t)) for t in range(KT)]
K_DMAS = [2 * len(heads_of_tile(t)) for t in range(KT)]
C_DMAS = [2 * len(pieces_of_head(h)) for h in range(H)]
C_DMAS_BATCH = [sum(C_DMAS[h] for h in range(par, H, 2)) for par in range(2)]


def context_dmas_before(h):
    return sum(C_DMAS[g] for g in range(h % 2, h, 2))


SHARED_USES = (["v0", "v1", "v2", "v3", "pv0", "wo0", "wo1", "pv1", "wo2", "wo3", "pv2",
                "q0", "pv3", "k0", "pv4", "q1", "pv5", "k1", "pv6", "q2", "k2", "pv7"])
PROLOGUE_USES = ["q0", "k0", "q1", "k1", "q2", "k2"]
PROJ_SLOT = {3: [("q", 0)], 4: [("k", 0)], 5: [("q", 1)], 6: [("k", 1)], 7: [("q", 2), ("k", 2)]}
WO_SLOT = {1: (0, 1), 2: (2, 3)}


def shared_bank(step, prologue=False):
    return (PROLOGUE_USES if prologue else SHARED_USES).index(step) % 2


def use_before(step, b):
    omitted = ("wo",) if isinstance(b, int) and b == 0 else ("q", "k") if isinstance(b, int) and b == LAST else ()
    at = SHARED_USES.index(step)
    for s in SHARED_USES[at % 2:at:2][::-1]:
        if not s.startswith(omitted or ("none",)):
            return s, False
    return (PROLOGUE_USES if isinstance(b, int) and b == 0 else SHARED_USES)[at % 2::2][-1], True


def wait_past(eng, sem, value):
    if isinstance(value, int) and value <= 0:
        return
    eng.wait_ge(sem, value)


def wait_apart(eng, sem, value, passed):
    if isinstance(value, int):
        wait_past(eng, sem, value)
    else:
        eng.compute_val(value)
        eng.wait_ge(passed, 1)
        eng.wait_ge(sem, value)


def attention_phase(nc, x, xT, adj, wq, bqT, wk, bkT, wv, bv, wo, bo, alpha1, gamma1, x1_dram):
    ctx = ExitStack()
    with ctx:
        def sb(name, shape, dt=FP32):
            return ctx.enter_context(nc.sbuf_tensor(name, shape, dt))

        def pb(name, shape):
            return ctx.enter_context(nc.psum_tensor(name, shape, FP32))

        def sem(name):
            return ctx.enter_context(nc.semaphore(name))

        w_hi = {n: sb(f"w{n}_hi", [P, KT, D], FP32R) for n in "qkvo"}
        w_lo = {n: sb(f"w{n}_lo", [P, KT, D], FP32R) for n in "qkvo"}
        raw = sb("raw", [P, KT * N])
        raw_T = raw[:, :].rearrange("p (k n) -> p k n", k=KT)
        raw_rows = raw[:, :].rearrange("p (t d) -> p t d", t=TT)
        xT_hi = sb("xT_hi", [P, KT, N], FP32R)
        xT_lo = sb("xT_lo", [P, KT, N], FP32R)
        x1 = sb("x1", [P, TT, D])
        stage_hi = {n: sb(f"stage_{n}_hi", [P, N], FP32R) for n in "qk"}
        stage_lo = {n: sb(f"stage_{n}_lo", [P, N], FP32R) for n in "qk"}
        q_hl = sb("q_hl", [2 * DH, H, N], FP32R)
        q_lh = sb("q_lh", [2 * DH, H, N], FP32R)
        k_hl = sb("k_hl", [2 * DH, H, N], FP32R)
        v_s = sb("v_s", [P, TT, H, V_COLS], FP32R)
        adj_raw = sb("adj_raw", [P, 2, N])
        adj_neg = sb("adj_neg", [P, TT, N])
        probs = sb("probs", [P, 2, TT, N])
        pT_hi = sb("pT_hi", [P, TT, TT, P], FP32R)
        pT_lo = sb("pT_lo", [P, TT, TT, P], FP32R)
        ctx_stage = sb("ctx_stage", [P, 2, N])
        ctx_a = sb("ctx_a", [P, 2, N])
        ctx_b = sb("ctx_b", [P, 2, N])
        ctx_hi = sb("ctx_hi", [P, KT, N], FP32R)
        ctx_lo = sb("ctx_lo", [P, KT, N], FP32R)
        squares = sb("squares", [P, D])
        bo_b = sb("bo_b", [P, D])
        alpha_b = sb("alpha_b", [P, D])
        gamma_b = sb("gamma_b", [P, D])
        bq_c = sb("bq_c", [P, KT])
        bk_c = sb("bk_c", [P, KT])
        bv_c = sb("bv_c", [P, H])
        ident = sb("ident", [P, P])
        neg_max = sb("neg_max", [P, 2 * TT])
        row_sum = sb("row_sum", [P, 2 * TT])
        inv_sum = sb("inv_sum", [P, 2 * TT])
        sum_sq = sb("sum_sq", [P, TT])
        mean_sq = sb("mean_sq", [P, TT])
        rstd = sb("rstd", [P, TT])
        minus_half = sb("minus_half", [P, TT])

        ps_s = [pb(f"ps_s{i}", [P, N]) for i in range(2)]
        ps_t = [pb(f"ps_t{i}", [P, 2, N]) for i in range(2)]
        ps_g = [pb(f"ps_g{i}", [P, N]) for i in range(2)]

        w_loaded = {n: sem(f"w{n}_loaded") for n in "qkvo"}
        consts_loaded = sem("consts_loaded")
        xT_loaded = sem("xT_loaded")
        rows_loaded = sem("rows_loaded")
        adj_loaded = [sem(f"adj_loaded{i}") for i in range(2)]
        zeroed = sem("zeroed")
        consts_ready = sem("consts_ready")
        w_step = sem("w_step")
        wo_step = sem("wo_step")
        w_ready = {n: sem(f"w{n}_split") for n in "qkvo"}
        xT_hi_done = sem("xT_hi_done")
        xT_split = sem("xT_split")
        adj_negated = sem("adj_negated")
        proj_ready = sem("proj_ready")
        proj_hi = sem("proj_hi")
        proj_lo = sem("proj_lo")
        q_stacked = [sem(f"q_stacked{t}") for t in range(KT)]
        k_stacked = [sem(f"k_stacked{t}") for t in range(KT)]
        v_ready = sem("v_ready")
        v_hi_done = sem("v_hi_done")
        v_lo_done = sem("v_lo_done")
        scores_ready = sem("scores_ready")
        logits_ready = sem("logits_ready")
        exp_done = sem("exp_done")
        inv_done = sem("inv_done")
        probs_ready = sem("probs_ready")
        transposed = sem("transposed")
        pT_hi_done = sem("pT_hi_done")
        pT_lo_done = sem("pT_lo_done")
        pv_ready = sem("pv_ready")
        ctx_staged = sem("ctx_staged")
        ctx_moved = [sem(f"ctx_moved{i}") for i in range(2)]
        ctx_summed = sem("ctx_summed")
        ctx_hi_done = sem("ctx_hi_done")
        ctx_split = sem("ctx_split")
        wo_ready = sem("wo_ready")
        xbo_ready = sem("xbo_ready")
        resid_ready = sem("resid_ready")
        squared = sem("squared")
        mean_ready = sem("mean_ready")
        rstd_ready = sem("rstd_ready")
        scaled = sem("scaled")
        x1_ready = sem("x1_ready")
        x1_stored = sem("x1_stored")
        bq_scaled = sem("bq_scaled")

        def score_no(b, h, qt):
            return H * TT * b + TT * h + qt + 1

        def pair_no(b, h, pair):
            return 2 * H * b + 2 * h + pair + 1

        def proj_no(b, kind, t):
            return 2 * KT * b + 2 * t + "qk".index(kind) + 1

        block = ctx.enter_context(nc.Block())

        @block.sync
        def _(sp):
            def load_xT(b):
                sp.dma_start(raw_T, xT[b].rearrange("(k p) n -> p k n", p=P)).then_inc(xT_loaded, DMA)

            def load_adj(b, qt):
                wait_past(sp, adj_negated, TT * b + qt + 1 - 2)
                sp.dma_start(adj_raw[:, qt % 2, :], adj[b, qt * P:(qt + 1) * P, :])\
                  .then_inc(adj_loaded[qt % 2], DMA)

            def stack_projection(b, kind, t, earlier):
                if earlier is not None:
                    wait_apart(sp, scores_ready, score_no(earlier, heads_of_tile(t)[-1], TT - 1), zeroed)
                sp.wait_ge(proj_lo, proj_no(b, kind, t))
                for h in heads_of_tile(t):
                    for tile, src, dst, n in pieces_of_head(h):
                        if tile != t:
                            continue
                        hi = stage_hi[kind][src:src + n, :].bitcast(FP32)
                        lo = stage_lo[kind][src:src + n, :].bitcast(FP32)
                        if kind == "q":
                            sp.dma_start(q_hl[dst:dst + n, h, :].bitcast(FP32), hi).then_inc(q_stacked[t], DMA)
                            sp.dma_start(q_hl[DH + dst:DH + dst + n, h, :].bitcast(FP32), lo).then_inc(q_stacked[t], DMA)
                            sp.dma_start(q_lh[dst:dst + n, h, :].bitcast(FP32), lo).then_inc(q_stacked[t], DMA)
                            sp.dma_start(q_lh[DH + dst:DH + dst + n, h, :].bitcast(FP32), hi).then_inc(q_stacked[t], DMA)
                        else:
                            sp.dma_start(k_hl[dst:dst + n, h, :].bitcast(FP32), hi).then_inc(k_stacked[t], DMA)
                            sp.dma_start(k_hl[DH + dst:DH + dst + n, h, :].bitcast(FP32), lo).then_inc(k_stacked[t], DMA)

            def move_context(b, h):
                wait_apart(sp, ctx_staged, H * b + h + 1, zeroed)
                for t, dst, src, n in pieces_of_head(h):
                    wait_past(sp, ctx_split, KT * b + t + 1 - (2 if t == 2 else 1 if t == 0 else KT))
                    sp.dma_start(ctx_a[dst:dst + n, t % 2, :], ctx_stage[src:src + n, h % 2, :])\
                      .then_inc(ctx_moved[h % 2], DMA)
                    sp.dma_start(ctx_b[dst:dst + n, t % 2, :], ctx_stage[LO + src:LO + src + n, h % 2, :])\
                      .then_inc(ctx_moved[h % 2], DMA)

            def store_x1(b):
                sp.wait_ge(x1_ready, TT * b + TT)
                sp.dma_start(x1_dram[b].rearrange("(t p) d -> p t d", p=P), x1[:, :, :])\
                  .then_inc(x1_stored, DMA)

            def batch(b, first=False, last=False):
                for h in range(H):
                    if h == 0 and not last:
                        wait_past(sp, xbo_ready, TT * b)
                        load_xT(b + 1)
                    if h == 1 and not last:
                        load_adj(b + 1, 0)
                        load_adj(b + 1, 1)
                    if h == 3:
                        sp.wait_ge(xT_split, KT * B if last else KT * (b + 2))
                        sp.dma_start(raw_rows, x[b].rearrange("(t p) d -> p t d", p=P))\
                          .then_inc(rows_loaded, DMA)
                    if h == 4 and not first:
                        store_x1(b - 1)
                    if h == 7 and not last:
                        load_adj(b + 1, 2)
                        load_adj(b + 1, 3)
                    if not last:
                        for kind, t in PROJ_SLOT.get(h, ()):
                            stack_projection(b + 1, kind, t, b)
                    move_context(b, h)

            wide = probs[:, :, :, :].rearrange("p a t n -> p (a t n)")
            for i, (n, w) in enumerate((("q", wq), ("k", wk), ("v", wv))):
                sp.dma_start(wide[:, i * KT * D:(i + 1) * KT * D].rearrange("p (k n) -> p k n", k=KT),
                             w.rearrange("(k p) n -> p k n", p=P)).then_inc(w_loaded[n], DMA)
                if n == "q":
                    load_xT(0)
            sp.wait_ge(zeroed, 1)
            sp.dma_start(bq_c[:, :], bqT).then_inc(consts_loaded, DMA)
            sp.dma_start(bk_c[:, :], bkT).then_inc(consts_loaded, DMA)
            sp.dma_start(bv_c[0:DH, :], bv).then_inc(consts_loaded, DMA)
            load_adj(0, 0)
            load_adj(0, 1)
            sp.dma_start(x1[:, 0:KT, :], wo.rearrange("(k p) n -> p k n", p=P)).then_inc(w_loaded["o"], DMA)
            sp.dma_start(bo_b[:, :], bo.partition_broadcast(P)).then_inc(consts_loaded, DMA)
            sp.dma_start(alpha_b[:, :], alpha1.partition_broadcast(P)).then_inc(consts_loaded, DMA)
            sp.dma_start(gamma_b[:, :], gamma1.partition_broadcast(P)).then_inc(consts_loaded, DMA)
            load_adj(0, 2)
            load_adj(0, 3)
            for kind, t in (("q", 0), ("k", 0), ("q", 1), ("k", 1), ("q", 2), ("k", 2)):
                stack_projection(0, kind, t, None)
            batch(0, first=True)
            with sp.Fori(1, LAST) as b:
                batch(b)
            batch(LAST, last=True)
            store_x1(LAST)
            sp.wait_ge(x1_stored, DMA * B)

        @block.gpsimd
        def _(pool):
            def split_xT(b, k):
                wait_apart(pool, xT_loaded, DMA * (b + 1), consts_ready)
                wait_apart(pool, v_ready, TT * b, consts_ready)
                pool.tensor_copy(xT_hi[:, k, :], raw_T[:, k, :]).then_inc(xT_hi_done, 1)
                pool.wait_ge(xT_hi_done, KT * b + k + 1)
                pool.tensor_tensor(xT_lo[:, k, :], raw_T[:, k, :], xT_hi[:, k, :].bitcast(FP32),
                                   ALU.subtract).then_inc(xT_split, 1)

            def negate_adj(b, qt):
                pool.wait_ge(adj_loaded[qt % 2], DMA * (2 * b + qt // 2 + 1))
                if not isinstance(b, int) or b > 0:
                    wait_apart(pool, logits_ready, score_no(b - 1, H - 1, qt), consts_ready)
                pool.tensor_scalar(adj_neg[:, qt, :], adj_raw[:, qt % 2, :], -1.0, None, ALU.mult)\
                    .then_inc(adj_negated, 1)

            def normalise(b, h, pair):
                wait_apart(pool, inv_done, pair_no(b, h, pair), consts_ready)
                for qt in (2 * pair, 2 * pair + 1):
                    at = h % 2 * TT + qt
                    pool.tensor_scalar(probs[:, h % 2, qt, :], probs[:, h % 2, qt, :],
                                       inv_sum[:, at:at + 1], None, ALU.mult).then_inc(probs_ready, 1)

            def split_context(b, t):
                heads = heads_of_tile(t)
                for par in range(2):
                    g = [h for h in heads if h % 2 == par][-1]
                    pool.wait_ge(ctx_moved[par], DMA * (C_DMAS_BATCH[par] * b
                                                        + context_dmas_before(g) + C_DMAS[g]))
                pool.tensor_tensor(ctx_a[:, t % 2, :], ctx_a[:, t % 2, :], ctx_b[:, t % 2, :], ALU.add)\
                    .then_inc(ctx_summed, 1)
                wait_past(pool, wo_ready, TT * b)
                wait_apart(pool, ctx_summed, KT * b + t + 1, consts_ready)
                pool.tensor_copy(ctx_hi[:, t, :], ctx_a[:, t % 2, :]).then_inc(ctx_hi_done, 1)
                pool.wait_ge(ctx_hi_done, KT * b + t + 1)
                pool.tensor_tensor(ctx_lo[:, t, :], ctx_a[:, t % 2, :], ctx_hi[:, t, :].bitcast(FP32),
                                   ALU.subtract).then_inc(ctx_split, 1)

            def add_bo(b, t):
                pool.wait_ge(rows_loaded, DMA * (b + 1))
                wait_past(pool, x1_stored, DMA * b)
                pool.tensor_tensor(x1[:, t, :], raw_rows[:, t, :], bo_b[:, :], ALU.add)\
                    .then_inc(xbo_ready, 1)

            def inverse_rms(b, pair):
                s = slice(2 * pair, 2 * pair + 2)
                wait_apart(pool, squared, TT * b + 2 * pair + 2, consts_ready)
                pool.tensor_scalar(mean_sq[:, s], sum_sq[:, s], 1.0 / D, EPS_RMS, ALU.mult, ALU.add)\
                    .then_inc(mean_ready, 1)
                pool.wait_ge(mean_ready, 2 * b + pair + 1)
                pool.tensor_tensor(rstd[:, s], mean_sq[:, s], minus_half[:, s], ALU.pow)\
                    .then_inc(rstd_ready, 1)

            def add_gamma(b, t):
                pool.wait_ge(scaled, TT * b + t + 1)
                pool.tensor_tensor(x1[:, t, :], x1[:, t, :], gamma_b[:, :], ALU.add).then_inc(x1_ready, 1)

            def batch(b, first=False, last=False):
                for h in range(H):
                    if h == 0 and not first:
                        split_context(b - 1, 2)
                    if h == 1 and not last:
                        split_xT(b + 1, 0)
                        split_xT(b + 1, 1)
                    if h == 2:
                        if not first:
                            inverse_rms(b - 1, 0)
                        if not last:
                            split_xT(b + 1, 2)
                    if h == 3 and not first:
                        inverse_rms(b - 1, 1)
                        add_gamma(b - 1, 0)
                        add_gamma(b - 1, 1)
                    if h == 4:
                        if not first:
                            add_gamma(b - 1, 2)
                            add_gamma(b - 1, 3)
                        split_context(b, 0)
                    if h == 5:
                        add_bo(b, 0)
                        add_bo(b, 1)
                        add_bo(b, 2)
                    if h == 6:
                        add_bo(b, 3)
                        split_context(b, 1)
                    if h == 7 and not last:
                        for qt in range(TT):
                            negate_adj(b + 1, qt)
                    if h + 1 < H:
                        normalise(b, h + 1, 0)
                        normalise(b, h + 1, 1)
                    elif not last:
                        normalise(b + 1, 0, 0)
                        normalise(b + 1, 0, 1)

            pool.memset(bv_c[:, :], 0.0).then_inc(zeroed, 1)
            pool.memset(minus_half[:, :], -0.5).then_inc(consts_ready, 1)
            pool.memset(v_s[:, :, :, DH:LO].bitcast(FP32), 0.0).then_inc(consts_ready, 1)
            pool.memset(ident[:, :], 0.0).then_inc(consts_ready, 1)
            pool.wait_ge(consts_ready, 3)
            pool.affine_select(out=ident[:, :], in_=ident[:, :], compare_op=ALU.not_equal, fill=1.0,
                               base=0, pattern=[[-1, P]], channel_multiplier=1).then_inc(consts_ready, 1)
            for k in range(KT):
                split_xT(0, k)
            for qt in range(TT):
                negate_adj(0, qt)
            pool.wait_ge(w_loaded["o"], DMA)
            pool.tensor_copy(w_hi["o"][:, :, :], x1[:, 0:KT, :]).then_inc(wo_step, 1)
            pool.wait_ge(wo_step, 1)
            pool.tensor_tensor(w_lo["o"][:, :, :], x1[:, 0:KT, :], w_hi["o"][:, :, :].bitcast(FP32),
                               ALU.subtract).then_inc(w_ready["o"], 1)
            pool.wait_ge(w_ready["o"], 1)
            pool.wait_ge(consts_loaded, 6 * DMA)
            normalise(0, 0, 0)
            normalise(0, 0, 1)
            batch(0, first=True)
            with pool.Fori(1, LAST) as b:
                batch(b)
            batch(LAST, last=True)
            split_context(LAST, 2)
            inverse_rms(LAST, 0)
            inverse_rms(LAST, 1)
            for t in range(TT):
                add_gamma(LAST, t)

        @block.scalar
        def _(act):
            def project_hi(b, kind, t, bank):
                act.wait_ge(proj_ready, proj_no(b, kind, t))
                moved, dmas = (q_stacked, Q_DMAS) if kind == "q" else (k_stacked, K_DMAS)
                if t > 0:
                    act.wait_ge(moved[t - 1], DMA * dmas[t - 1] * (b + 1))
                else:
                    wait_past(act, moved[KT - 1], DMA * dmas[KT - 1] * b)
                bias = bq_c if kind == "q" else bk_c
                nc.scalar.activation(stage_hi[kind][:, :], ps_g[bank][:, :], ACT.Identity,
                                     bias=bias[:, t:t + 1]).then_inc(proj_hi, 1)

            def v_hi(b, kt):
                act.wait_ge(v_ready, TT * b + kt + 1)
                wait_past(act, pv_ready, H * b)
                nc.scalar.activation(v_s[:, kt, :, 0:DH],
                                     ps_g[shared_bank(f"v{kt}")][:, 0:D].rearrange("p (h d) -> p h d", h=H),
                                     ACT.Copy)\
                  .then_inc(v_hi_done, 1)

            def exponent(b, h, qt):
                at = h % 2 * TT + qt
                act.wait_ge(logits_ready, score_no(b, h, qt))
                nc.scalar.activation(probs[:, h % 2, qt, :], probs[:, h % 2, qt, :], ACT.Exp, scale=-1.0,
                                     bias=neg_max[:, at:at + 1], accum_out=row_sum[:, at:at + 1])\
                  .then_inc(exp_done, 1)

            def pT_high(b, h, pair):
                act.wait_ge(transposed, pair_no(b, h, pair))
                wait_past(act, pv_ready, H * b + h)
                nc.scalar.activation(pT_hi[:, 2 * pair:2 * pair + 2, :, :],
                                     ps_t[pair][:, :, :].rearrange("p q (k i) -> p q k i", k=TT), ACT.Copy)\
                  .then_inc(pT_hi_done, 1)

            def stage_context(b, h):
                act.wait_ge(pv_ready, H * b + h + 1)
                wait_past(act, ctx_moved[h % 2], DMA * (C_DMAS_BATCH[h % 2] * b + context_dmas_before(h)))
                bank = shared_bank(f"pv{h}")
                nc.scalar.activation(ctx_stage[0:V_COLS, h % 2, :], ps_g[bank][0:V_COLS, :], ACT.Identity,
                                     bias=bv_c[0:V_COLS, h:h + 1]).then_inc(ctx_staged, 1)

            def square(b, t):
                act.wait_ge(resid_ready, TT * b + t + 1)
                wait_past(act, squared, TT * b + t)
                nc.scalar.activation(squares[:, :], x1[:, t, :], ACT.Square,
                                     accum_out=sum_sq[:, t:t + 1]).then_inc(squared, 1)

            def batch(b, first=False, last=False):
                for kt in range(TT):
                    v_hi(b, kt)
                for h in range(H):
                    more = h + 1 < H or not last
                    nb, nh = (b, h + 1) if h + 1 < H else (b + 1, 0)
                    pT_high(b, h, 0)
                    if more:
                        exponent(nb, nh, 0)
                        exponent(nb, nh, 1)
                    pT_high(b, h, 1)
                    if more:
                        exponent(nb, nh, 2)
                        exponent(nb, nh, 3)
                    if not first:
                        for t in WO_SLOT.get(h, ()):
                            square(b - 1, t)
                    if not last:
                        for kind, t in PROJ_SLOT.get(h, ()):
                            project_hi(b + 1, kind, t, shared_bank(f"{kind}{t}"))
                    stage_context(b, h)

            act.wait_ge(consts_loaded, 6 * DMA)
            act.wait_ge(consts_ready, 4)
            act.wait_ge(bq_scaled, 1)
            for kind, t in (("q", 0), ("k", 0), ("q", 1), ("k", 1), ("q", 2), ("k", 2)):
                project_hi(0, kind, t, shared_bank(f"{kind}{t}", prologue=True))
            for qt in range(TT):
                exponent(0, 0, qt)
            batch(0, first=True)
            with act.Fori(1, LAST) as b:
                batch(b)
            batch(LAST, last=True)
            for t in range(TT):
                square(LAST, t)

        @block.vector
        def _(dve):
            def project_lo(b, kind, t, bank):
                dve.wait_ge(proj_hi, proj_no(b, kind, t))
                bias = bq_c if kind == "q" else bk_c
                nc.vector.scalar_tensor_tensor(out=stage_lo[kind][:, :], in0=ps_g[bank][:, :],
                                               scalar=bias[:, t:t + 1], in1=stage_hi[kind][:, :].bitcast(FP32),
                                               op0=ALU.add, op1=ALU.subtract).then_inc(proj_lo, 1)

            def v_lo(b, kt):
                dve.wait_ge(v_hi_done, TT * b + kt + 1)
                nc.vector.tensor_tensor(v_s[:, kt, :, LO:V_COLS],
                                        ps_g[shared_bank(f"v{kt}")][:, 0:D].rearrange("p (h d) -> p h d", h=H),
                                        v_s[:, kt, :, 0:DH].bitcast(FP32), ALU.subtract).then_inc(v_lo_done, 1)

            def logits(b, h, qt):
                at = h % 2 * TT + qt
                wait_apart(dve, scores_ready, score_no(b, h, qt), consts_loaded)
                if h == 0:
                    wait_apart(dve, adj_negated, TT * b + qt + 1, consts_loaded)
                wait_apart(dve, transposed, pair_no(b, h, qt // 2) - 4, consts_loaded)
                nc.vector.tensor_tensor_reduce(out=probs[:, h % 2, qt, :], in0=ps_s[qt % 2][:, :],
                                               in1=adj_neg[:, qt, :], scale=1.0, scalar=BIG,
                                               op0=ALU.add, op1=ALU.min,
                                               accum_out=neg_max[:, at:at + 1]).then_inc(logits_ready, 1)

            def invert_sums(b, h, pair):
                at = h % 2 * TT + 2 * pair
                dve.wait_ge(exp_done, score_no(b, h, 2 * pair + 1))
                nc.vector.reciprocal(inv_sum[:, at:at + 2], row_sum[:, at:at + 2]).then_inc(inv_done, 1)

            def pT_low(b, h, pair):
                dve.wait_ge(pT_hi_done, pair_no(b, h, pair))
                s = slice(2 * pair, 2 * pair + 2)
                nc.vector.tensor_tensor(pT_lo[:, s, :, :].rearrange("p q k i -> p (q k i)"),
                                        ps_t[pair][:, :, :].rearrange("p q n -> p (q n)"),
                                        pT_hi[:, s, :, :].rearrange("p q k i -> p (q k i)").bitcast(FP32),
                                        ALU.subtract).then_inc(pT_lo_done, 1)

            def residual(b, t):
                dve.wait_ge(wo_ready, TT * b + t + 1)
                dve.wait_ge(xbo_ready, TT * b + t + 1)
                nc.vector.tensor_tensor(x1[:, t, :], ps_g[shared_bank(f"wo{t}")][:, 0:D], x1[:, t, :], ALU.add)\
                    .then_inc(resid_ready, 1)

            def scale_rows(b, t):
                dve.wait_ge(rstd_ready, 2 * b + t // 2 + 1)
                nc.vector.scalar_tensor_tensor(out=x1[:, t, :], in0=x1[:, t, :], scalar=rstd[:, t:t + 1],
                                               in1=alpha_b[:, :], op0=ALU.mult, op1=ALU.mult)\
                    .then_inc(scaled, 1)

            def batch(b, first=False, last=False):
                for kt in range(TT):
                    v_lo(b, kt)
                for h in range(H):
                    more = h + 1 < H or not last
                    nb, nh = (b, h + 1) if h + 1 < H else (b + 1, 0)
                    pT_low(b, h, 0)
                    if more:
                        logits(nb, nh, 0)
                        logits(nb, nh, 1)
                    pT_low(b, h, 1)
                    if more:
                        invert_sums(nb, nh, 0)
                        logits(nb, nh, 2)
                        logits(nb, nh, 3)
                    if not first:
                        for t in WO_SLOT.get(h, ()):
                            residual(b - 1, t)
                        if h in (2, 3):
                            scale_rows(b - 1, 2 * (h - 2))
                            scale_rows(b - 1, 2 * (h - 2) + 1)
                    if not last:
                        for kind, t in PROJ_SLOT.get(h, ()):
                            project_lo(b + 1, kind, t, shared_bank(f"{kind}{t}"))
                    if more:
                        invert_sums(nb, nh, 1)

            wide = probs[:, :, :, :].rearrange("p a t n -> p (a t n)")
            steps = 0
            for i, n in enumerate("qkv"):
                w_raw = wide[:, i * KT * D:(i + 1) * KT * D]
                dve.wait_ge(w_loaded[n], DMA)
                if n == "q":
                    nc.vector.tensor_scalar(w_raw, w_raw, -DH ** -0.5, None, ALU.mult).then_inc(w_step, 1)
                    steps += 1
                    dve.wait_ge(w_step, steps)
                hi, lo = (w[n][:, :, :].rearrange("p k n -> p (k n)") for w in (w_hi, w_lo))
                nc.vector.tensor_copy(hi, w_raw).then_inc(w_step, 1)
                steps += 1
                dve.wait_ge(w_step, steps)
                nc.vector.tensor_tensor(lo, w_raw, hi.bitcast(FP32), ALU.subtract).then_inc(w_ready[n], 1)
                if n == "q":
                    dve.wait_ge(consts_loaded, 6 * DMA)
                    nc.vector.tensor_scalar(bq_c[:, :], bq_c[:, :], -DH ** -0.5, None, ALU.mult)\
                        .then_inc(bq_scaled, 1)
            dve.wait_ge(bq_scaled, 1)
            dve.wait_ge(w_ready["v"], 1)
            for kind, t in (("q", 0), ("k", 0), ("q", 1), ("k", 1), ("q", 2), ("k", 2)):
                project_lo(0, kind, t, shared_bank(f"{kind}{t}", prologue=True))
            for qt in range(TT):
                logits(0, 0, qt)
            invert_sums(0, 0, 0)
            invert_sums(0, 0, 1)
            batch(0, first=True)
            with dve.Fori(1, LAST) as b:
                batch(b)
            batch(LAST, last=True)
            for t in range(TT):
                residual(LAST, t)
            for t in range(TT):
                scale_rows(LAST, t)

        @block.tensor
        def _(pe):
            def wait_for_bank(step, b):
                user, iteration_before = use_before(step, b)
                it = b - 1 if iteration_before else b
                no = int(user[-1])
                if user.startswith("v"):
                    pe.wait_ge(v_lo_done, TT * it + no + 1)
                elif user.startswith("pv"):
                    pe.wait_ge(ctx_staged, H * it + no + 1)
                elif user.startswith("wo"):
                    pe.wait_ge(resid_ready, TT * (it - 1) + no + 1)
                else:
                    pe.wait_ge(proj_lo, proj_no(it + 1, user[0], no))

            def three_passes(out, pairs, done):
                n = 0
                for (a_hi, a_lo), (b_hi, b_lo) in pairs:
                    for lhsT, rhs in ((a_hi, b_hi), (a_hi, b_lo), (a_lo, b_hi)):
                        last = nc.tensor.matmul(out, lhsT=lhsT, rhs=rhs, start=(n == 0),
                                                stop=(n == 3 * len(pairs) - 1))
                        n += 1
                last.then_inc(done, 1)

            def project(b, kind, t, bank):
                cols = slice(t * P, (t + 1) * P)
                three_passes(ps_g[bank][:, :],
                             [((w_hi[kind][:, k, cols], w_lo[kind][:, k, cols]),
                               (xT_hi[:, k, :], xT_lo[:, k, :])) for k in range(KT)], proj_ready)

            def project_v(b, kt):
                wait_for_bank(f"v{kt}", b)
                toks = slice(kt * P, (kt + 1) * P)
                three_passes(ps_g[shared_bank(f"v{kt}")][:, 0:D],
                             [((xT_hi[:, k, toks], xT_lo[:, k, toks]),
                               (w_hi["v"][:, k, :], w_lo["v"][:, k, :])) for k in range(KT)], v_ready)

            def scores(b, h, qt):
                if qt == 0:
                    for t, *_ in pieces_of_head(h):
                        pe.wait_ge(q_stacked[t], DMA * Q_DMAS[t] * (b + 1))
                        pe.wait_ge(k_stacked[t], DMA * K_DMAS[t] * (b + 1))
                if score_first(b, h, qt) is None:
                    pe.wait_ge(logits_ready, score_no(b, h, qt) - 2)
                toks = slice(qt * P, (qt + 1) * P)
                nc.tensor.matmul(ps_s[qt % 2][:, :], lhsT=q_hl[:, h, toks], rhs=k_hl[:, h, :],
                                 start=True, stop=False)
                nc.tensor.matmul(ps_s[qt % 2][:, :], lhsT=q_lh[:, h, toks], rhs=k_hl[:, h, :],
                                 start=False, stop=True).then_inc(scores_ready, 1)

            def score_first(b, h, qt):
                return True if isinstance(b, int) and b == 0 and h == 0 and qt < 2 else None

            def transpose_probs(b, h, pair):
                pe.wait_ge(probs_ready, score_no(b, h, 2 * pair + 1))
                wait_past(pe, pT_lo_done, pair_no(b, h, pair) - 2)
                for j in range(2):
                    for kt in range(TT):
                        last = nc.tensor.transpose(ps_t[pair][:, j, kt * P:(kt + 1) * P],
                                                   probs[:, h % 2, 2 * pair + j, kt * P:(kt + 1) * P],
                                                   ident[:, :])
                last.then_inc(transposed, 1)

            def attend(b, h):
                wait_for_bank(f"pv{h}", b)
                if h == 0:
                    pe.wait_ge(v_lo_done, TT * b + TT)
                pe.wait_ge(pT_lo_done, pair_no(b, h, 1))
                out = ps_g[shared_bank(f"pv{h}")][0:V_COLS, :]
                for kt in range(TT):
                    v_head = v_s[:, kt, h, :]
                    for part, pT in enumerate((pT_hi, pT_lo)):
                        last = nc.tensor.matmul(out, lhsT=v_head, rhs=pT[:, :, kt, :],
                                                start=(kt == 0 and part == 0), stop=(kt == TT - 1 and part == 1))
                last.then_inc(pv_ready, 1)

            def project_out(b, t):
                toks = slice(t * P, (t + 1) * P)
                three_passes(ps_g[shared_bank(f"wo{t}")][:, 0:D],
                             [((ctx_hi[:, k, toks], ctx_lo[:, k, toks]),
                               (w_hi["o"][:, k, :], w_lo["o"][:, k, :])) for k in range(KT)], wo_ready)

            def batch(b, first=False, last=False):
                for kt in range(TT):
                    project_v(b, kt)
                for h in range(H):
                    more = h + 1 < H or not last
                    nb, nh = (b, h + 1) if h + 1 < H else (b + 1, 0)
                    transpose_probs(b, h, 0)
                    if more:
                        scores(nb, nh, 0)
                        scores(nb, nh, 1)
                    transpose_probs(b, h, 1)
                    if more:
                        scores(nb, nh, 2)
                        scores(nb, nh, 3)
                    if not first:
                        for t in WO_SLOT.get(h, ()):
                            if t == 0:
                                pe.wait_ge(ctx_split, KT * b)
                            wait_for_bank(f"wo{t}", b)
                            project_out(b - 1, t)
                    if not last:
                        for kind, t in PROJ_SLOT.get(h, ()):
                            if t == 0:
                                pe.wait_ge(xT_split, KT * (b + 2))
                            wait_for_bank(f"{kind}{t}", b)
                            project(b + 1, kind, t, shared_bank(f"{kind}{t}"))
                    attend(b, h)

            pe.wait_ge(consts_ready, 4)
            pe.wait_ge(xT_split, KT)
            for i, (kind, t) in enumerate((("q", 0), ("k", 0), ("q", 1), ("k", 1), ("q", 2), ("k", 2))):
                pe.wait_ge(w_ready[kind], 1)
                if i >= 2:
                    pe.wait_ge(proj_lo, i - 1)
                project(0, kind, t, shared_bank(f"{kind}{t}", prologue=True))
            for qt in range(TT):
                scores(0, 0, qt)
            pe.wait_ge(w_ready["v"], 1)
            batch(0, first=True)
            pe.wait_ge(w_ready["o"], 1)
            with pe.Fori(1, LAST) as b:
                batch(b)
            batch(LAST, last=True)
            pe.wait_ge(ctx_split, KT * B)
            for t in range(TT):
                bank = shared_bank(f"wo{t}")
                pe.wait_ge(ctx_staged, H * B)
                for earlier in range(t):
                    if shared_bank(f"wo{earlier}") == bank:
                        pe.wait_ge(resid_ready, TT * LAST + earlier + 1)
                project_out(LAST, t)


def feed_forward_phase(nc, x, w1, b1T, w2, b2, alpha2, gamma2, x1_dram, out):
    ctx = ExitStack()
    with ctx:
        def sb(name, shape, dt=FP32):
            return ctx.enter_context(nc.sbuf_tensor(name, shape, dt))

        def pb(name, shape):
            return ctx.enter_context(nc.psum_tensor(name, shape, FP32))

        def sem(name):
            return ctx.enter_context(nc.semaphore(name))

        BUFS = 3
        w1_hi = sb("w1_hi", [P, KT, F], FP32R)
        w1_lo = sb("w1_lo", [P, KT, F], FP32R)
        w2_hi = sb("w2_hi", [P, JT, D], FP32R)
        w2_lo = sb("w2_lo", [P, JT, D], FP32R)
        w1_raw = sb("w1_raw", [P, KT, F])
        w2_raw = sb("w2_raw", [P, JT, D])
        x1_rows = sb("x1_rows", [P, TT, D])
        x1T_hi = sb("x1T_hi", [P, KT, N], FP32R)
        x1T_lo = sb("x1T_lo", [P, KT, N], FP32R)
        hidden = sb("hidden", [P, BUFS, N])
        h_hi = sb("h_hi", [P, JT, N], FP32R)
        h_lo = sb("h_lo", [P, JT, N], FP32R)
        y = sb("y", [P, TT, D])
        z = sb("z", [P, TT, D])
        b1_c = sb("b1_c", [P, JT])
        b2_b = sb("b2_b", [P, D])
        alpha_b = sb("alpha2_b", [P, D])
        gamma_b = sb("gamma2_b", [P, D])
        ident = sb("ident2", [P, P])
        squares = sb("squares2", [P, D])
        sum_sq = sb("sum_sq2", [P, TT])
        mean_sq = sb("mean_sq2", [P, TT])
        rms = sb("rms2", [P, TT])
        stats = sb("stats", [P, TT, 6])
        mean_var = sb("mean_var", [P, TT, 2])
        var_eps = sb("var_eps", [P, TT])
        inv_std = sb("inv_std", [P, TT])
        minus_half = sb("minus_half2", [P, TT])

        ps_h = [pb(f"ps_h{i}", [P, N]) for i in range(BUFS)]
        ps_x = [pb(f"ps_x{i}", [P, N]) for i in range(KT)]
        ps_y = [pb(f"ps_y{i}", [P, N]) for i in range(2)]

        w1_loaded = sem("w1_loaded")
        w2_loaded = sem("w2_loaded")
        consts_loaded = sem("consts2_loaded")
        consts_ready = sem("consts2_ready")
        x1_loaded = sem("x1_loaded")
        rows_loaded = sem("rows2_loaded")
        w_step = sem("w12_step")
        w1_ready = sem("w1_ready")
        w2_ready = sem("w2_ready")
        x1_transposed = sem("x1_transposed")
        x1T_hi_done = sem("x1T_hi_done")
        x1T_lo_done = sem("x1T_lo_done")
        up_ready = sem("up_ready")
        hidden_ready = sem("hidden_ready")
        h_hi_done = sem("h_hi_done")
        h_lo_done = sem("h_lo_done")
        down_ready = sem("down_ready")
        xb2_ready = sem("xb2_ready")
        xg_ready = sem("xg_ready")
        resid_ready = sem("resid2_ready")
        squared = sem("squared2")
        mean_ready = sem("mean2_ready")
        rms_ready = sem("rms_ready")
        normed = sem("normed")
        summed = sem("summed")
        stats_done = sem("stats_done")
        aggregated = sem("aggregated")
        var_ready = sem("var_ready")
        inv_std_ready = sem("inv_std_ready")
        out_ready = sem("out_ready")
        out_stored = sem("out_stored")

        block = ctx.enter_context(nc.Block())

        @block.sync
        def _(sp):
            def rows(ap):
                return ap.rearrange("(t p) d -> p t d", p=P)

            def batch(b, first=False, last=False):
                wait_past(sp, out_stored, DMA * TT * b)
                sp.dma_start(z[:, :, :], rows(x[b])).then_inc(rows_loaded, DMA)
                if not last:
                    wait_apart(sp, x1_transposed, KT * (b + 1), rows_loaded)
                    wait_apart(sp, xb2_ready, TT * (b + 1), rows_loaded)
                    sp.dma_start(x1_rows[:, :, :], rows(x1_dram[b + 1])).then_inc(x1_loaded, DMA)
                for t in range(TT):
                    store(b, t)

            def store(b, t):
                sp.wait_ge(out_ready, TT * b + t + 1)
                sp.dma_start(out[b, t * P:(t + 1) * P, :], z[:, t, :]).then_inc(out_stored, DMA)

            sp.dma_start(x1_rows[:, :, :], rows(x1_dram[0])).then_inc(x1_loaded, DMA)
            for k in range(KT):
                sp.dma_start(w1_raw[:, k, :], w1[k * P:(k + 1) * P, :]).then_inc(w1_loaded, DMA)
            sp.dma_start(b1_c[:, :], b1T).then_inc(consts_loaded, DMA)
            sp.dma_start(w2_raw[:, :, :], w2.rearrange("(j p) d -> p j d", p=P)).then_inc(w2_loaded, DMA)
            sp.dma_start(b2_b[:, :], b2.partition_broadcast(P)).then_inc(consts_loaded, DMA)
            sp.dma_start(alpha_b[:, :], alpha2.partition_broadcast(P)).then_inc(consts_loaded, DMA)
            sp.dma_start(gamma_b[:, :], gamma2.partition_broadcast(P)).then_inc(consts_loaded, DMA)
            batch(0, first=True)
            with sp.Fori(1, LAST) as b:
                batch(b)
            batch(LAST, last=True)
            sp.wait_ge(out_stored, DMA * TT * B)

        @block.gpsimd
        def _(pool):
            def inverse_rms(b, t):
                wait_apart(pool, squared, TT * b + t + 1, consts_ready)
                pool.tensor_scalar(mean_sq[:, t:t + 1], sum_sq[:, t:t + 1], 1.0 / D, EPS_RMS,
                                   ALU.mult, ALU.add).then_inc(mean_ready, 1)
                pool.wait_ge(mean_ready, TT * b + t + 1)
                pool.tensor_tensor(rms[:, t:t + 1], mean_sq[:, t:t + 1], minus_half[:, t:t + 1], ALU.pow)\
                    .then_inc(rms_ready, 1)

            def inverse_std(b, t):
                wait_apart(pool, aggregated, TT * b + t + 1, consts_ready)
                pool.tensor_scalar(var_eps[:, t:t + 1], mean_var[:, t, 1:2], EPS_LN, None, ALU.add)\
                    .then_inc(var_ready, 1)
                pool.wait_ge(var_ready, TT * b + t + 1)
                pool.tensor_tensor(inv_std[:, t:t + 1], var_eps[:, t:t + 1], minus_half[:, t:t + 1], ALU.pow)\
                    .then_inc(inv_std_ready, 1)

            def batch(b, first=False, last=False):
                if not first:
                    inverse_std(b - 1, TT - 1)
                pool.wait_ge(x1_loaded, DMA * (b + 1))
                wait_past(pool, summed, TT * b)
                for t in range(TT):
                    pool.tensor_tensor(y[:, t, :], x1_rows[:, t, :], b2_b[:, :], ALU.add)\
                        .then_inc(xb2_ready, 1)
                pool.wait_ge(rows_loaded, DMA * (b + 1))
                for t in range(TT):
                    pool.tensor_tensor(z[:, t, :], z[:, t, :], gamma_b[:, :], ALU.add).then_inc(xg_ready, 1)
                for t in range(TT):
                    inverse_rms(b, t)
                    if t > 0:
                        inverse_std(b, t - 1)

            pool.memset(minus_half[:, :], -0.5).then_inc(consts_ready, 1)
            pool.memset(ident[:, :], 0.0).then_inc(consts_ready, 1)
            pool.wait_ge(consts_ready, 2)
            pool.affine_select(out=ident[:, :], in_=ident[:, :], compare_op=ALU.not_equal, fill=1.0,
                               base=0, pattern=[[-1, P]], channel_multiplier=1).then_inc(consts_ready, 1)
            pool.wait_ge(w2_loaded, DMA)
            pool.tensor_copy(w2_hi[:, :, :], w2_raw[:, :, :]).then_inc(w2_ready, 1)
            pool.wait_ge(w2_ready, 1)
            pool.tensor_tensor(w2_lo[:, :, :], w2_raw[:, :, :], w2_hi[:, :, :].bitcast(FP32), ALU.subtract)\
                .then_inc(w2_ready, 1)
            pool.wait_ge(consts_loaded, 4 * DMA)
            batch(0, first=True)
            with pool.Fori(1, LAST) as b:
                batch(b)
            batch(LAST, last=True)
            inverse_std(LAST, TT - 1)

        @block.scalar
        def _(act):
            def x1T_high(b, k):
                act.wait_ge(x1_transposed, KT * b + k + 1)
                wait_past(act, up_ready, JT * b)
                nc.scalar.activation(x1T_hi[:, k, :], ps_x[k][:, :], ACT.Copy).then_inc(x1T_hi_done, 1)

            def batch(b, last=False):
                for j in range(JT):
                    act.wait_ge(up_ready, JT * b + j + 1)
                    wait_past(act, h_lo_done, JT * b + j + 1 - BUFS)
                    nc.scalar.activation(hidden[:, j % BUFS, :], ps_h[j % BUFS][:, :], ACT.Silu,
                                         bias=b1_c[:, j:j + 1]).then_inc(hidden_ready, 1)
                if not last:
                    for k in range(KT):
                        x1T_high(b + 1, k)
                for t in range(TT):
                    act.wait_ge(resid_ready, TT * b + t + 1)
                    wait_past(act, squared, TT * b + t)
                    nc.scalar.activation(squares[:, :], y[:, t, :], ACT.Square,
                                         accum_out=sum_sq[:, t:t + 1]).then_inc(squared, 1)

            for k in range(KT):
                x1T_high(0, k)
            act.wait_ge(consts_loaded, 4 * DMA)
            batch(0)
            with act.Fori(1, LAST) as b:
                batch(b)
            batch(LAST, last=True)

        @block.vector
        def _(dve):
            def x1T_low(b, k):
                dve.wait_ge(x1T_hi_done, KT * b + k + 1)
                nc.vector.tensor_tensor(x1T_lo[:, k, :], ps_x[k][:, :], x1T_hi[:, k, :].bitcast(FP32),
                                        ALU.subtract).then_inc(x1T_lo_done, 1)

            def residual(b, t):
                dve.wait_ge(down_ready, TT * b + t + 1)
                dve.wait_ge(xb2_ready, TT * b + t + 1)
                nc.vector.tensor_tensor(y[:, t, :], ps_y[t % 2][:, 0:D], y[:, t, :], ALU.add)\
                    .then_inc(resid_ready, 1)

            def second_sum(b, t):
                dve.wait_ge(rms_ready, TT * b + t + 1)
                nc.vector.scalar_tensor_tensor(out=y[:, t, :], in0=y[:, t, :], scalar=rms[:, t:t + 1],
                                               in1=alpha_b[:, :], op0=ALU.mult, op1=ALU.mult).then_inc(normed, 1)
                dve.wait_ge(xg_ready, TT * b + t + 1)
                dve.wait_ge(normed, TT * b + t + 1)
                nc.vector.tensor_tensor(z[:, t, :], y[:, t, :], z[:, t, :], ALU.add).then_inc(summed, 1)
                dve.wait_ge(summed, TT * b + t + 1)
                nc.vector.bn_stats(stats[:, t, :], z[:, t, :]).then_inc(stats_done, 1)
                wait_apart(dve, stats_done, TT * b + t + 1, consts_loaded)
                nc.vector.bn_aggr(mean_var[:, t, :], stats[:, t, :]).then_inc(aggregated, 1)

            def finish(b, t):
                dve.wait_ge(inv_std_ready, TT * b + t + 1)
                nc.vector.tensor_scalar(z[:, t, :], z[:, t, :], mean_var[:, t, 0:1], inv_std[:, t:t + 1],
                                        ALU.subtract, ALU.mult).then_inc(out_ready, 1)

            def batch(b, first=False, last=False):
                for j in range(JT):
                    if j == 0:
                        wait_past(dve, down_ready, TT * b)
                    dve.wait_ge(hidden_ready, JT * b + j + 1)
                    nc.vector.tensor_copy(h_hi[:, j, :], hidden[:, j % BUFS, :]).then_inc(h_hi_done, 1)
                    dve.wait_ge(h_hi_done, JT * b + j + 1)
                    nc.vector.tensor_tensor(h_lo[:, j, :], hidden[:, j % BUFS, :], h_hi[:, j, :].bitcast(FP32),
                                            ALU.subtract).then_inc(h_lo_done, 1)
                    if j == 1 and not first:
                        second_sum(b - 1, TT - 1)
                        finish(b - 1, TT - 2)
                    if j == 3 and not first:
                        finish(b - 1, TT - 1)
                if not last:
                    for k in range(KT):
                        x1T_low(b + 1, k)
                for t in range(TT):
                    residual(b, t)
                    if t >= 1:
                        second_sum(b, t - 1)
                    if t >= 2:
                        finish(b, t - 2)

            for k in range(KT):
                dve.wait_ge(w1_loaded, KT * DMA)
                nc.vector.tensor_copy(w1_hi[:, k, :], w1_raw[:, k, :]).then_inc(w_step, 1)
                dve.wait_ge(w_step, k + 1)
                nc.vector.tensor_tensor(w1_lo[:, k, :], w1_raw[:, k, :], w1_hi[:, k, :].bitcast(FP32),
                                        ALU.subtract).then_inc(w1_ready, 1)
            dve.wait_ge(consts_loaded, 4 * DMA)
            for k in range(KT):
                x1T_low(0, k)
            batch(0, first=True)
            with dve.Fori(1, LAST) as b:
                batch(b)
            batch(LAST, last=True)
            second_sum(LAST, TT - 1)
            finish(LAST, TT - 2)
            finish(LAST, TT - 1)

        @block.tensor
        def _(pe):
            def three_passes(out_ps, pairs, done):
                n = 0
                for (a_hi, a_lo), (b_hi, b_lo) in pairs:
                    for lhsT, rhs in ((a_hi, b_hi), (a_hi, b_lo), (a_lo, b_hi)):
                        last = nc.tensor.matmul(out_ps, lhsT=lhsT, rhs=rhs, start=(n == 0),
                                                stop=(n == 3 * len(pairs) - 1))
                        n += 1
                last.then_inc(done, 1)

            def transpose_x1(b, k):
                wait_past(pe, x1T_lo_done, KT * b + k + 1 - KT)
                for t in range(TT):
                    last = nc.tensor.transpose(ps_x[k][:, t * P:(t + 1) * P], x1_rows[:, t, k * P:(k + 1) * P],
                                               ident[:, :])
                last.then_inc(x1_transposed, 1)

            def batch(b, last=False):
                pe.wait_ge(x1T_lo_done, KT * (b + 1))
                for j in range(JT):
                    wait_past(pe, hidden_ready, JT * b + j + 1 - BUFS)
                    cols = slice(j * P, (j + 1) * P)
                    three_passes(ps_h[j % BUFS][:, :],
                                 [((w1_hi[:, k, cols], w1_lo[:, k, cols]), (x1T_hi[:, k, :], x1T_lo[:, k, :]))
                                  for k in range(KT)], up_ready)
                if not last:
                    pe.wait_ge(x1_loaded, DMA * (b + 2))
                    for k in range(KT):
                        transpose_x1(b + 1, k)
                for t in range(TT):
                    wait_past(pe, resid_ready, TT * b + t + 1 - 2)
                    toks = slice(t * P, (t + 1) * P)
                    n = 0
                    for j in range(JT):
                        if t == 0:
                            pe.wait_ge(h_lo_done, JT * b + j + 1)
                        for lhsT, rhs in ((h_hi[:, j, toks], w2_hi[:, j, :]), (h_hi[:, j, toks], w2_lo[:, j, :]),
                                          (h_lo[:, j, toks], w2_hi[:, j, :])):
                            end = nc.tensor.matmul(ps_y[t % 2][:, 0:D], lhsT=lhsT, rhs=rhs, start=(n == 0),
                                                   stop=(n == 3 * JT - 1))
                            n += 1
                    end.then_inc(down_ready, 1)

            pe.wait_ge(consts_ready, 3)
            pe.wait_ge(x1_loaded, DMA)
            for k in range(KT):
                transpose_x1(0, k)
            pe.wait_ge(w1_ready, KT)
            pe.wait_ge(w2_ready, 2)
            batch(0)
            with pe.Fori(1, LAST) as b:
                batch(b)
            batch(LAST, last=True)


def transformer_layer(nc, x, xT, adj, wq, bqT, wk, bkT, wv, bv, wo, bo, w1, b1T, w2, b2,
                      alpha1, gamma1, alpha2, gamma2, out):
    x1_dram = nc.dram_tensor("x1_rows_dram", (B, N, D), FP32, kind="Internal").ap()
    attention_phase(nc, x, xT, adj, wq, bqT, wk, bkT, wv, bv, wo, bo, alpha1, gamma1, x1_dram)
    feed_forward_phase(nc, x, w1, b1T, w2, b2, alpha2, gamma2, x1_dram, out)


def kernel(x, adj, **layer):
    import numpy as _np
    import concourse.bacc as _bacc
    from concourse.bass_utils import run_bass_kernel_spmd as _run

    w = {name.removeprefix("L0_gnn_"): _np.asarray(a) for name, a in layer.items()}
    x = _np.asarray(x)

    def per_partition(v, tiles):
        return v.reshape(tiles, -1).T

    ins = [("x", x), ("xT", x.transpose(0, 2, 1)), ("adj", _np.asarray(adj)),
           ("wq", w["wq"]), ("bqT", per_partition(w["bq"], KT)),
           ("wk", w["wk"]), ("bkT", per_partition(w["bk"], KT)),
           ("wv", w["wv"]), ("bv", per_partition(w["bv"], H)),
           ("wo", w["wo"]), ("bo", w["bo"]), ("w1", w["w1"]), ("b1T", per_partition(w["b1"], JT)),
           ("w2", w["w2"]), ("b2", w["b2"]), ("alpha1", w["alpha1"]), ("gamma1", w["gamma1"]),
           ("alpha2", w["alpha2"]), ("gamma2", w["gamma2"])]
    nc = _bacc.Bacc("TRN2", target_bir_lowering=False, num_devices=1)
    arrays, args = {}, []
    for name, a in ins:
        arrays[f"in_{name}"] = _np.ascontiguousarray(a)
        args.append(nc.dram_tensor(f"in_{name}", a.shape, mybir.dt.from_np(a.dtype), kind="ExternalInput").ap())
    args.append(nc.dram_tensor("out_0", (B, N, D), FP32, kind="ExternalOutput").ap())
    transformer_layer(nc, *args)
    r = _run(nc, [arrays], core_ids=[0])
    return r.results[0]["out_0"]
```

```python
from contextlib import ExitStack

import concourse.bass as bass
from concourse import mybir

FP32 = mybir.dt.float32
FP32R = mybir.dt.float32r
ALU = mybir.AluOpType
ACT = mybir.ActivationFunctionType

P = 128
B, N, D = 16, 512, 384
H = 8
DH = D // H
F = 1536
TT = N // P
KT = D // P
JT = F // P
LAST = B - 1
EPS_RMS = 1e-6
EPS_LN = 1e-5
BIG = 3.0e38
DMA = 16


def pieces_of_head(h):
    out, f, end = [], h * DH, (h + 1) * DH
    while f < end:
        t = f // P
        n = min(end, (t + 1) * P) - f
        out.append((t, f - t * P, f - h * DH, n))
        f += n
    return out


def heads_of_tile(t):
    return [h for h in range(H) if any(p[0] == t for p in pieces_of_head(h))]


LO = 64
V_COLS = LO + DH

Q_DMAS = [4 * len(heads_of_tile(t)) for t in range(KT)]
K_DMAS = [2 * len(heads_of_tile(t)) for t in range(KT)]
C_DMAS = [2 * len(pieces_of_head(h)) for h in range(H)]
C_DMAS_BATCH = [sum(C_DMAS[h] for h in range(par, H, 2)) for par in range(2)]


def context_dmas_before(h):
    return sum(C_DMAS[g] for g in range(h % 2, h, 2))


PAIRS = 2 * H
AHEAD = 3
SIDE = {0: ["v0", "v1"], 1: ["v2", "v3"], 2: ["q2"], 3: ["k2"], 4: ["wo0"], 5: ["wo1"], 6: ["wo2"],
        7: ["wo3"], 8: ["q0"], 9: ["k0"], 11: ["q1"], 13: ["k1"]}
PROLOGUE_USES = ["q0", "k0", "q1", "k1"]
SHARED_USES = [s for p in range(PAIRS) for s in ([f"pv{(p // 2 - 1) % H}"] if p % 2 == 0 else []) + SIDE.get(p, [])]
assert len(SHARED_USES) % 2 == 0 and len(PROLOGUE_USES) % 2 == 0


def left_out(step, b):
    if not isinstance(b, int):
        return False
    return (b == 0 and (step == "pv7" or step.startswith("wo"))
            or b == LAST and step in PROLOGUE_USES)


def batch_of(step, b):
    if step == "pv7" or step.startswith("wo"):
        return b - 1
    return b + 1 if step in PROLOGUE_USES else b


def shared_bank(step, prologue=False):
    return (PROLOGUE_USES if prologue else SHARED_USES).index(step) % 2


def use_before(step, b):
    at = SHARED_USES.index(step)
    for s in SHARED_USES[at % 2:at:2][::-1]:
        if not left_out(s, b):
            return s, batch_of(s, b)
    if isinstance(b, int) and b == 0:
        return PROLOGUE_USES[at % 2::2][-1], 0
    s = [s for s in SHARED_USES[at % 2::2] if not left_out(s, b - 1)][-1]
    return s, batch_of(s, b - 1)


def steps_of(p, b, kinds):
    return [(s, s[:-1], int(s[-1])) for s in SIDE.get(p, []) if s[:-1] in kinds and not left_out(s, b)]


def pair_at(b, p):
    return (b, p // 2, p % 2) if p < PAIRS else (b + 1, (p - PAIRS) // 2, p % 2)


def wait_past(eng, sem, value):
    if isinstance(value, int) and value <= 0:
        return
    eng.wait_ge(sem, value)


def wait_apart(eng, sem, value, passed):
    if isinstance(value, int):
        wait_past(eng, sem, value)
    else:
        eng.compute_val(value)
        eng.wait_ge(passed, 1)
        eng.wait_ge(sem, value)


def attention_phase(nc, x, xT, adj, wq, bqT, wk, bkT, wv, bv, wo, bo, alpha1, gamma1, x1_dram):
    ctx = ExitStack()
    with ctx:
        def sb(name, shape, dt=FP32):
            return ctx.enter_context(nc.sbuf_tensor(name, shape, dt))

        def pb(name, shape):
            return ctx.enter_context(nc.psum_tensor(name, shape, FP32))

        def sem(name):
            return ctx.enter_context(nc.semaphore(name))

        w_hi = {n: sb(f"w{n}_hi", [P, KT, D], FP32R) for n in "qkvo"}
        w_lo = {n: sb(f"w{n}_lo", [P, KT, D], FP32R) for n in "qkvo"}
        raw = sb("raw", [P, KT * N])
        raw_T = raw[:, :].rearrange("p (k n) -> p k n", k=KT)
        raw_rows = raw[:, :].rearrange("p (t d) -> p t d", t=TT)
        xT_hi = sb("xT_hi", [P, KT, N], FP32R)
        xT_lo = sb("xT_lo", [P, KT, N], FP32R)
        x1 = sb("x1", [P, TT, D])
        stage_hi = {n: sb(f"stage_{n}_hi", [P, N], FP32R) for n in "qk"}
        stage_lo = {n: sb(f"stage_{n}_lo", [P, N], FP32R) for n in "qk"}
        q_hl = sb("q_hl", [2 * DH, H, N], FP32R)
        q_lh = sb("q_lh", [2 * DH, H, N], FP32R)
        k_hl = sb("k_hl", [2 * DH, H, N], FP32R)
        v_s = sb("v_s", [P, TT, H, V_COLS], FP32R)
        adj_s = sb("adj_s", [P, TT, N])
        adj_first = sb("adj_first", [P, 2, N])
        probs = sb("probs", [P, 8, N])
        pT_hi = sb("pT_hi", [P, TT, TT, P], FP32R)
        pT_lo = sb("pT_lo", [P, TT, TT, P], FP32R)
        ctx_stage = sb("ctx_stage", [P, 2, N])
        ctx_a = sb("ctx_a", [P, 2, N])
        ctx_b = sb("ctx_b", [P, 2, N])
        ctx_hi = sb("ctx_hi", [P, KT, N], FP32R)
        ctx_lo = sb("ctx_lo", [P, KT, N], FP32R)
        squares = sb("squares", [P, D])
        bo_b = sb("bo_b", [P, D])
        alpha_b = sb("alpha_b", [P, D])
        gamma_b = sb("gamma_b", [P, D])
        bq_c = sb("bq_c", [P, KT])
        bk_c = sb("bk_c", [P, KT])
        bv_c = sb("bv_c", [P, H])
        ident = sb("ident", [P, P])
        row_max = sb("row_max", [P, 2 * TT])
        neg_max = sb("neg_max", [P, 2 * TT])
        row_sum = sb("row_sum", [P, 2 * TT])
        inv_sum = sb("inv_sum", [P, 2 * TT])
        sum_sq = sb("sum_sq", [P, TT])
        mean_sq = sb("mean_sq", [P, TT])
        rstd = sb("rstd", [P, TT])
        minus_half = sb("minus_half", [P, TT])

        ps_s = [pb(f"ps_s{i}", [P, N]) for i in range(2)]
        ps_t = [pb(f"ps_t{i}", [P, 2, N]) for i in range(2)]
        ps_g = [pb(f"ps_g{i}", [P, N]) for i in range(2)]

        w_loaded = {n: sem(f"w{n}_loaded") for n in "qkvo"}
        consts_loaded = sem("consts_loaded")
        xT_loaded = sem("xT_loaded")
        rows_loaded = sem("rows_loaded")
        adj_loaded = [sem(f"adj_loaded{i}") for i in range(2)]
        adj_first_loaded = sem("adj_first_loaded")
        zeroed = sem("zeroed")
        consts_ready = sem("consts_ready")
        w_step = sem("w_step")
        wo_step = sem("wo_step")
        w_ready = {n: sem(f"w{n}_split") for n in "qkvo"}
        xT_hi_done = sem("xT_hi_done")
        xT_split = sem("xT_split")
        proj_ready = sem("proj_ready")
        proj_hi = sem("proj_hi")
        proj_lo = sem("proj_lo")
        q_stacked = [sem(f"q_stacked{t}") for t in range(KT)]
        k_stacked = [sem(f"k_stacked{t}") for t in range(KT)]
        v_ready = sem("v_ready")
        v_hi_done = sem("v_hi_done")
        v_lo_done = sem("v_lo_done")
        scores_ready = sem("scores_ready")
        logits_ready = sem("logits_ready")
        neg_max_ready = sem("neg_max_ready")
        exp_done = sem("exp_done")
        inv_done = sem("inv_done")
        probs_ready = sem("probs_ready")
        transposed = sem("transposed")
        pT_hi_done = sem("pT_hi_done")
        pT_lo_done = sem("pT_lo_done")
        pv_ready = sem("pv_ready")
        ctx_staged = sem("ctx_staged")
        ctx_moved = [sem(f"ctx_moved{i}") for i in range(2)]
        ctx_summed = sem("ctx_summed")
        ctx_hi_done = sem("ctx_hi_done")
        ctx_split = sem("ctx_split")
        wo_ready = sem("wo_ready")
        xbo_ready = sem("xbo_ready")
        resid_ready = sem("resid_ready")
        squared = sem("squared")
        mean_ready = sem("mean_ready")
        rstd_ready = sem("rstd_ready")
        scaled = sem("scaled")
        x1_ready = sem("x1_ready")
        x1_stored = sem("x1_stored")
        bq_scaled = sem("bq_scaled")

        def score_no(b, h, qt):
            return H * TT * b + TT * h + qt + 1

        def ring(h, qt):
            return (TT * h + qt) % 8

        def pair_no(b, h, pair):
            return 2 * H * b + 2 * h + pair + 1

        def proj_no(b, kind, t):
            return 2 * KT * b + 2 * t + "qk".index(kind) + 1

        block = ctx.enter_context(nc.Block())

        @block.sync
        def _(sp):
            def load_xT(b):
                sp.dma_start(raw_T, xT[b].rearrange("(k p) n -> p k n", p=P)).then_inc(xT_loaded, DMA)

            def load_adj(tile, b, pair, loaded):
                rows = adj[b, 2 * pair * P:2 * (pair + 1) * P, :]
                sp.dma_start(tile, rows.rearrange("(t p) k -> p t k", p=P)).then_inc(loaded, DMA)

            def load_adj_pair(b, pair):
                wait_apart(sp, logits_ready, score_no(b - 1, H - 1, 2 * pair + 1), zeroed)
                load_adj(adj_s[:, 2 * pair:2 * pair + 2, :], b, pair, adj_loaded[pair])

            def stack_projection(b, kind, t, earlier):
                if not isinstance(earlier, int) or earlier >= 0:
                    wait_apart(sp, scores_ready, score_no(earlier, heads_of_tile(t)[-1], TT - 1), zeroed)
                sp.wait_ge(proj_lo, proj_no(b, kind, t))
                for h in heads_of_tile(t):
                    for tile, src, dst, n in pieces_of_head(h):
                        if tile != t:
                            continue
                        hi = stage_hi[kind][src:src + n, :].bitcast(FP32)
                        lo = stage_lo[kind][src:src + n, :].bitcast(FP32)
                        if kind == "q":
                            sp.dma_start(q_hl[dst:dst + n, h, :].bitcast(FP32), hi).then_inc(q_stacked[t], DMA)
                            sp.dma_start(q_hl[DH + dst:DH + dst + n, h, :].bitcast(FP32), lo).then_inc(q_stacked[t], DMA)
                            sp.dma_start(q_lh[dst:dst + n, h, :].bitcast(FP32), lo).then_inc(q_stacked[t], DMA)
                            sp.dma_start(q_lh[DH + dst:DH + dst + n, h, :].bitcast(FP32), hi).then_inc(q_stacked[t], DMA)
                        else:
                            sp.dma_start(k_hl[dst:dst + n, h, :].bitcast(FP32), hi).then_inc(k_stacked[t], DMA)
                            sp.dma_start(k_hl[DH + dst:DH + dst + n, h, :].bitcast(FP32), lo).then_inc(k_stacked[t], DMA)

            def move_context(b, h):
                wait_apart(sp, ctx_staged, H * b + h + 1, zeroed)
                for t, dst, src, n in pieces_of_head(h):
                    wait_past(sp, ctx_split, KT * b + t + 1 - (2 if t == 2 else 1 if t == 0 else KT))
                    sp.dma_start(ctx_a[dst:dst + n, t % 2, :], ctx_stage[src:src + n, h % 2, :])\
                      .then_inc(ctx_moved[h % 2], DMA)
                    sp.dma_start(ctx_b[dst:dst + n, t % 2, :], ctx_stage[LO + src:LO + src + n, h % 2, :])\
                      .then_inc(ctx_moved[h % 2], DMA)

            def store_x1(b):
                sp.wait_ge(x1_ready, TT * b + TT)
                sp.dma_start(x1_dram[b].rearrange("(t p) d -> p t d", p=P), x1[:, :, :])\
                  .then_inc(x1_stored, DMA)

            def batch(b, first=False, last=False):
                for p in range(PAIRS):
                    if p == 0 and not last:
                        wait_past(sp, xbo_ready, TT * b)
                        load_xT(b + 1)
                    if p == 1 and not last:
                        wait_apart(sp, logits_ready, score_no(b, 0, 1), zeroed)
                        load_adj(adj_first[:, :, :], b + 1, 0, adj_first_loaded)
                    if p == 9:
                        sp.wait_ge(xT_split, KT * B if last else KT * (b + 2))
                        sp.dma_start(raw_rows, x[b].rearrange("(t p) d -> p t d", p=P))\
                          .then_inc(rows_loaded, DMA)
                    if p == 12 and not first:
                        store_x1(b - 1)
                    if p in (12, 13) and not last:
                        load_adj_pair(b + 1, p - 12)
                    for step, kind, t in steps_of(p, b, "qk"):
                        of = batch_of(step, b)
                        stack_projection(of, kind, t, of - 1)
                    if p % 2 == 0 and not (first and p == 0):
                        move_context(*((b, p // 2 - 1) if p else (b - 1, H - 1)))

            wide = probs[:, :, :].rearrange("p a n -> p (a n)")
            for i, (n, w) in enumerate((("q", wq), ("k", wk), ("v", wv))):
                sp.dma_start(wide[:, i * KT * D:(i + 1) * KT * D].rearrange("p (k n) -> p k n", k=KT),
                             w.rearrange("(k p) n -> p k n", p=P)).then_inc(w_loaded[n], DMA)
                if n == "q":
                    load_xT(0)
            sp.wait_ge(zeroed, 1)
            sp.dma_start(bq_c[:, :], bqT).then_inc(consts_loaded, DMA)
            sp.dma_start(bk_c[:, :], bkT).then_inc(consts_loaded, DMA)
            sp.dma_start(bv_c[0:DH, :], bv).then_inc(consts_loaded, DMA)
            load_adj(adj_first[:, :, :], 0, 0, adj_first_loaded)
            load_adj(adj_s[:, 2:4, :], 0, 1, adj_loaded[1])
            load_adj(adj_s[:, 0:2, :], 0, 0, adj_loaded[0])
            sp.dma_start(x1[:, 0:KT, :], wo.rearrange("(k p) n -> p k n", p=P)).then_inc(w_loaded["o"], DMA)
            sp.dma_start(bo_b[:, :], bo.partition_broadcast(P)).then_inc(consts_loaded, DMA)
            sp.dma_start(alpha_b[:, :], alpha1.partition_broadcast(P)).then_inc(consts_loaded, DMA)
            sp.dma_start(gamma_b[:, :], gamma1.partition_broadcast(P)).then_inc(consts_loaded, DMA)
            for step in PROLOGUE_USES:
                stack_projection(0, step[0], int(step[1]), -1)
            batch(0, first=True)
            with sp.Fori(1, LAST) as b:
                batch(b)
            batch(LAST, last=True)
            move_context(LAST, H - 1)
            store_x1(LAST)
            sp.wait_ge(x1_stored, DMA * B)

        @block.gpsimd
        def _(pool):
            def split_xT(b, k):
                wait_apart(pool, xT_loaded, DMA * (b + 1), consts_ready)
                wait_apart(pool, proj_ready, 2 * KT * b, consts_ready)
                pool.tensor_copy(xT_hi[:, k, :], raw_T[:, k, :]).then_inc(xT_hi_done, 1)
                pool.wait_ge(xT_hi_done, KT * b + k + 1)
                pool.tensor_tensor(xT_lo[:, k, :], raw_T[:, k, :], xT_hi[:, k, :].bitcast(FP32),
                                   ALU.subtract).then_inc(xT_split, 1)

            def split_context(b, t):
                heads = heads_of_tile(t)
                for par in range(2):
                    g = [h for h in heads if h % 2 == par][-1]
                    pool.wait_ge(ctx_moved[par], DMA * (C_DMAS_BATCH[par] * b
                                                        + context_dmas_before(g) + C_DMAS[g]))
                pool.tensor_tensor(ctx_a[:, t % 2, :], ctx_a[:, t % 2, :], ctx_b[:, t % 2, :], ALU.add)\
                    .then_inc(ctx_summed, 1)
                wait_past(pool, wo_ready, TT * b)
                wait_apart(pool, ctx_summed, KT * b + t + 1, consts_ready)
                pool.tensor_copy(ctx_hi[:, t, :], ctx_a[:, t % 2, :]).then_inc(ctx_hi_done, 1)
                pool.wait_ge(ctx_hi_done, KT * b + t + 1)
                pool.tensor_tensor(ctx_lo[:, t, :], ctx_a[:, t % 2, :], ctx_hi[:, t, :].bitcast(FP32),
                                   ALU.subtract).then_inc(ctx_split, 1)

            def add_bo(b, t):
                pool.wait_ge(rows_loaded, DMA * (b + 1))
                wait_past(pool, x1_stored, DMA * b)
                pool.tensor_tensor(x1[:, t, :], raw_rows[:, t, :], bo_b[:, :], ALU.add)\
                    .then_inc(xbo_ready, 1)

            def inverse_rms(b, pair):
                s = slice(2 * pair, 2 * pair + 2)
                wait_apart(pool, squared, TT * b + 2 * pair + 2, consts_ready)
                pool.tensor_scalar(mean_sq[:, s], sum_sq[:, s], 1.0 / D, EPS_RMS, ALU.mult, ALU.add)\
                    .then_inc(mean_ready, 1)
                pool.wait_ge(mean_ready, 2 * b + pair + 1)
                pool.tensor_tensor(rstd[:, s], mean_sq[:, s], minus_half[:, s], ALU.pow)\
                    .then_inc(rstd_ready, 1)

            def add_gamma(b, t):
                pool.wait_ge(scaled, TT * b + t + 1)
                pool.tensor_tensor(x1[:, t, :], x1[:, t, :], gamma_b[:, :], ALU.add).then_inc(x1_ready, 1)

            def batch(b, first=False, last=False):
                for p in range(PAIRS):
                    if p == 2 and not first:
                        split_context(b - 1, 2)
                    if p in (4, 5, 6) and not last:
                        split_xT(b + 1, p - 4)
                    if p == 7 and not first:
                        inverse_rms(b - 1, 0)
                    if p == 8 and not first:
                        inverse_rms(b - 1, 1)
                        add_gamma(b - 1, 0)
                        add_gamma(b - 1, 1)
                    if p == 9:
                        split_context(b, 0)
                    if p == 11 and not first:
                        add_gamma(b - 1, 2)
                        add_gamma(b - 1, 3)
                    if p in (12, 13):
                        add_bo(b, 2 * (p - 12))
                        add_bo(b, 2 * (p - 12) + 1)
                    if p == 14:
                        split_context(b, 1)

            pool.memset(bv_c[:, :], 0.0).then_inc(zeroed, 1)
            pool.memset(minus_half[:, :], -0.5).then_inc(consts_ready, 1)
            pool.memset(v_s[:, :, :, DH:LO].bitcast(FP32), 0.0).then_inc(consts_ready, 1)
            pool.memset(ident[:, :], 0.0).then_inc(consts_ready, 1)
            pool.wait_ge(consts_ready, 3)
            pool.affine_select(out=ident[:, :], in_=ident[:, :], compare_op=ALU.not_equal, fill=1.0,
                               base=0, pattern=[[-1, P]], channel_multiplier=1).then_inc(consts_ready, 1)
            for k in range(KT):
                split_xT(0, k)
            pool.wait_ge(w_loaded["o"], DMA)
            pool.tensor_copy(w_hi["o"][:, :, :], x1[:, 0:KT, :]).then_inc(wo_step, 1)
            pool.wait_ge(wo_step, 1)
            pool.tensor_tensor(w_lo["o"][:, :, :], x1[:, 0:KT, :], w_hi["o"][:, :, :].bitcast(FP32),
                               ALU.subtract).then_inc(w_ready["o"], 1)
            pool.wait_ge(w_ready["o"], 1)
            pool.wait_ge(consts_loaded, 6 * DMA)
            batch(0, first=True)
            with pool.Fori(1, LAST) as b:
                batch(b)
            batch(LAST, last=True)
            split_context(LAST, 2)
            inverse_rms(LAST, 0)
            inverse_rms(LAST, 1)
            for t in range(TT):
                add_gamma(LAST, t)

        @block.scalar
        def _(act):
            def project_hi(b, kind, t, bank):
                act.wait_ge(proj_ready, proj_no(b, kind, t))
                moved, dmas = (q_stacked, Q_DMAS) if kind == "q" else (k_stacked, K_DMAS)
                if t > 0:
                    act.wait_ge(moved[t - 1], DMA * dmas[t - 1] * (b + 1))
                else:
                    wait_past(act, moved[KT - 1], DMA * dmas[KT - 1] * b)
                bias = bq_c if kind == "q" else bk_c
                nc.scalar.activation(stage_hi[kind][:, :], ps_g[bank][:, :], ACT.Identity,
                                     bias=bias[:, t:t + 1]).then_inc(proj_hi, 1)

            def v_hi(b, kt):
                act.wait_ge(v_ready, TT * b + kt + 1)
                wait_past(act, pv_ready, H * b)
                nc.scalar.activation(v_s[:, kt, :, 0:DH],
                                     ps_g[shared_bank(f"v{kt}")][:, 0:D].rearrange("p (h d) -> p h d", h=H),
                                     ACT.Copy)\
                  .then_inc(v_hi_done, 1)

            def exponent(b, h, qt):
                at = ring(h, qt)
                act.wait_ge(neg_max_ready, pair_no(b, h, qt // 2))
                nc.scalar.activation(probs[:, at, :], probs[:, at, :], ACT.Exp,
                                     bias=neg_max[:, at:at + 1], accum_out=row_sum[:, at:at + 1])\
                  .then_inc(exp_done, 1)

            def pT_high(b, h, pair):
                act.wait_ge(transposed, pair_no(b, h, pair))
                wait_past(act, pv_ready, H * b + h)
                nc.scalar.activation(pT_hi[:, 2 * pair:2 * pair + 2, :, :],
                                     ps_t[pair][:, :, :].rearrange("p q (k i) -> p q k i", k=TT), ACT.Copy)\
                  .then_inc(pT_hi_done, 1)

            def stage_context(b, h):
                act.wait_ge(pv_ready, H * b + h + 1)
                wait_past(act, ctx_moved[h % 2], DMA * (C_DMAS_BATCH[h % 2] * b + context_dmas_before(h)))
                bank = shared_bank(f"pv{h}")
                nc.scalar.activation(ctx_stage[0:V_COLS, h % 2, :], ps_g[bank][0:V_COLS, :], ACT.Identity,
                                     bias=bv_c[0:V_COLS, h:h + 1]).then_inc(ctx_staged, 1)

            def square(b, t):
                act.wait_ge(resid_ready, TT * b + t + 1)
                wait_past(act, squared, TT * b + t)
                nc.scalar.activation(squares[:, :], x1[:, t, :], ACT.Square,
                                     accum_out=sum_sq[:, t:t + 1]).then_inc(squared, 1)

            def batch(b, first=False, last=False):
                for p in range(PAIRS):
                    if not (last and p + AHEAD >= PAIRS):
                        nb, nh, pair = pair_at(b, p + AHEAD)
                        exponent(nb, nh, 2 * pair)
                        exponent(nb, nh, 2 * pair + 1)
                    if p % 2 == 0 and not (first and p == 0):
                        stage_context(*((b, p // 2 - 1) if p else (b - 1, H - 1)))
                    pT_high(b, p // 2, p % 2)
                    for step, kind, t in steps_of(p, b, ("v", "q", "k", "wo")):
                        if kind == "v":
                            v_hi(b, t)
                        elif kind == "wo":
                            square(b - 1, t)
                        else:
                            project_hi(batch_of(step, b), kind, t, shared_bank(step))

            act.wait_ge(consts_loaded, 6 * DMA)
            act.wait_ge(consts_ready, 4)
            act.wait_ge(bq_scaled, 1)
            for step in PROLOGUE_USES:
                project_hi(0, step[0], int(step[1]), shared_bank(step, prologue=True))
            for p in range(AHEAD):
                for qt in range(2 * (p % 2), 2 * (p % 2) + 2):
                    exponent(0, p // 2, qt)
            batch(0, first=True)
            with act.Fori(1, LAST) as b:
                batch(b)
            batch(LAST, last=True)
            stage_context(LAST, H - 1)
            for t in range(TT):
                square(LAST, t)

        @block.vector
        def _(dve):
            def project_lo(b, kind, t, bank):
                dve.wait_ge(proj_hi, proj_no(b, kind, t))
                bias = bq_c if kind == "q" else bk_c
                nc.vector.scalar_tensor_tensor(out=stage_lo[kind][:, :], in0=ps_g[bank][:, :],
                                               scalar=bias[:, t:t + 1], in1=stage_hi[kind][:, :].bitcast(FP32),
                                               op0=ALU.add, op1=ALU.subtract).then_inc(proj_lo, 1)

            def v_lo(b, kt):
                dve.wait_ge(v_hi_done, TT * b + kt + 1)
                nc.vector.tensor_tensor(v_s[:, kt, :, LO:V_COLS],
                                        ps_g[shared_bank(f"v{kt}")][:, 0:D].rearrange("p (h d) -> p h d", h=H),
                                        v_s[:, kt, :, 0:DH].bitcast(FP32), ALU.subtract).then_inc(v_lo_done, 1)

            def logits(b, h, pair):
                for qt in (2 * pair, 2 * pair + 1):
                    at = ring(h, qt)
                    rows = adj_first[:, qt, :] if h == 0 and pair == 0 else adj_s[:, qt, :]
                    wait_apart(dve, scores_ready, score_no(b, h, qt), consts_loaded)
                    if h == 0 and pair == 0:
                        wait_apart(dve, adj_first_loaded, DMA * (b + 1), consts_loaded)
                    elif h == 0 or h == 1 and pair == 0:
                        wait_apart(dve, adj_loaded[pair], DMA * (b + 1), consts_loaded)
                    wait_apart(dve, transposed, pair_no(b, h, pair) - 4, consts_loaded)
                    nc.vector.tensor_tensor_reduce(out=probs[:, at, :], in0=ps_s[qt % 2][:, :],
                                                   in1=rows, scale=1.0, scalar=-BIG,
                                                   op0=ALU.add, op1=ALU.max,
                                                   accum_out=row_max[:, at:at + 1]).then_inc(logits_ready, 1)

            def negate_max(b, h, pair):
                at = ring(h, 2 * pair)
                dve.wait_ge(logits_ready, score_no(b, h, 2 * pair + 1))
                nc.vector.tensor_scalar(neg_max[:, at:at + 2], row_max[:, at:at + 2], -1.0, None, ALU.mult)\
                    .then_inc(neg_max_ready, 1)

            def normalise(b, h, pair):
                at = ring(h, 2 * pair)
                dve.wait_ge(exp_done, score_no(b, h, 2 * pair + 1))
                nc.vector.reciprocal(inv_sum[:, at:at + 2], row_sum[:, at:at + 2]).then_inc(inv_done, 1)
                dve.wait_ge(inv_done, pair_no(b, h, pair))
                for i in (at, at + 1):
                    nc.vector.tensor_scalar(probs[:, i, :], probs[:, i, :], inv_sum[:, i:i + 1], None,
                                            ALU.mult).then_inc(probs_ready, 1)

            def pT_low(b, h, pair):
                dve.wait_ge(pT_hi_done, pair_no(b, h, pair))
                s = slice(2 * pair, 2 * pair + 2)
                nc.vector.tensor_tensor(pT_lo[:, s, :, :].rearrange("p q k i -> p (q k i)"),
                                        ps_t[pair][:, :, :].rearrange("p q n -> p (q n)"),
                                        pT_hi[:, s, :, :].rearrange("p q k i -> p (q k i)").bitcast(FP32),
                                        ALU.subtract).then_inc(pT_lo_done, 1)

            def residual(b, t):
                dve.wait_ge(wo_ready, TT * b + t + 1)
                dve.wait_ge(xbo_ready, TT * b + t + 1)
                nc.vector.tensor_tensor(x1[:, t, :], ps_g[shared_bank(f"wo{t}")][:, 0:D], x1[:, t, :], ALU.add)\
                    .then_inc(resid_ready, 1)

            def scale_rows(b, t):
                dve.wait_ge(rstd_ready, 2 * b + t // 2 + 1)
                nc.vector.scalar_tensor_tensor(out=x1[:, t, :], in0=x1[:, t, :], scalar=rstd[:, t:t + 1],
                                               in1=alpha_b[:, :], op0=ALU.mult, op1=ALU.mult)\
                    .then_inc(scaled, 1)

            def batch(b, first=False, last=False):
                for p in range(PAIRS):
                    if not (last and p + AHEAD >= PAIRS):
                        ahead = pair_at(b, p + AHEAD)
                        logits(*ahead)
                        negate_max(*ahead)
                    if not (last and p + AHEAD - 1 >= PAIRS):
                        normalise(*pair_at(b, p + AHEAD - 1))
                    pT_low(b, p // 2, p % 2)
                    for step, kind, t in steps_of(p, b, ("v", "q", "k", "wo")):
                        if kind == "v":
                            v_lo(b, t)
                        elif kind == "wo":
                            residual(b - 1, t)
                        else:
                            project_lo(batch_of(step, b), kind, t, shared_bank(step))
                    if p in (8, 10) and not first:
                        scale_rows(b - 1, p - 8)
                        scale_rows(b - 1, p - 7)

            wide = probs[:, :, :].rearrange("p a n -> p (a n)")
            steps = 0
            for i, n in enumerate("qkv"):
                w_raw = wide[:, i * KT * D:(i + 1) * KT * D]
                dve.wait_ge(w_loaded[n], DMA)
                if n == "q":
                    nc.vector.tensor_scalar(w_raw, w_raw, DH ** -0.5, None, ALU.mult).then_inc(w_step, 1)
                    steps += 1
                    dve.wait_ge(w_step, steps)
                hi, lo = (w[n][:, :, :].rearrange("p k n -> p (k n)") for w in (w_hi, w_lo))
                nc.vector.tensor_copy(hi, w_raw).then_inc(w_step, 1)
                steps += 1
                dve.wait_ge(w_step, steps)
                nc.vector.tensor_tensor(lo, w_raw, hi.bitcast(FP32), ALU.subtract).then_inc(w_ready[n], 1)
                if n == "q":
                    dve.wait_ge(consts_loaded, 6 * DMA)
                    nc.vector.tensor_scalar(bq_c[:, :], bq_c[:, :], DH ** -0.5, None, ALU.mult)\
                        .then_inc(bq_scaled, 1)
            dve.wait_ge(bq_scaled, 1)
            dve.wait_ge(w_ready["v"], 1)
            for step in PROLOGUE_USES:
                project_lo(0, step[0], int(step[1]), shared_bank(step, prologue=True))
            for p in range(AHEAD):
                logits(0, p // 2, p % 2)
                negate_max(0, p // 2, p % 2)
            for p in range(AHEAD - 1):
                normalise(0, p // 2, p % 2)
            batch(0, first=True)
            with dve.Fori(1, LAST) as b:
                batch(b)
            batch(LAST, last=True)
            for t in range(TT):
                residual(LAST, t)
            for t in range(TT):
                scale_rows(LAST, t)

        @block.tensor
        def _(pe):
            def wait_for_bank(step, b):
                user, of = use_before(step, b)
                kind, no = user[:-1], int(user[-1])
                if kind == "v":
                    pe.wait_ge(v_lo_done, TT * of + no + 1)
                elif kind == "pv":
                    pe.wait_ge(ctx_staged, H * of + no + 1)
                elif kind == "wo":
                    pe.wait_ge(resid_ready, TT * of + no + 1)
                else:
                    pe.wait_ge(proj_lo, proj_no(of, kind, no))

            def three_passes(out, pairs, done):
                n = 0
                for (a_hi, a_lo), (b_hi, b_lo) in pairs:
                    for lhsT, rhs in ((a_hi, b_hi), (a_hi, b_lo), (a_lo, b_hi)):
                        last = nc.tensor.matmul(out, lhsT=lhsT, rhs=rhs, start=(n == 0),
                                                stop=(n == 3 * len(pairs) - 1))
                        n += 1
                last.then_inc(done, 1)

            def project(b, kind, t, bank):
                cols = slice(t * P, (t + 1) * P)
                three_passes(ps_g[bank][:, :],
                             [((w_hi[kind][:, k, cols], w_lo[kind][:, k, cols]),
                               (xT_hi[:, k, :], xT_lo[:, k, :])) for k in range(KT)], proj_ready)

            def project_v(b, kt):
                toks = slice(kt * P, (kt + 1) * P)
                three_passes(ps_g[shared_bank(f"v{kt}")][:, 0:D],
                             [((xT_hi[:, k, toks], xT_lo[:, k, toks]),
                               (w_hi["v"][:, k, :], w_lo["v"][:, k, :])) for k in range(KT)], v_ready)

            def scores(b, h, qt):
                if qt == 0:
                    for t, *_ in pieces_of_head(h):
                        pe.wait_ge(q_stacked[t], DMA * Q_DMAS[t] * (b + 1))
                        pe.wait_ge(k_stacked[t], DMA * K_DMAS[t] * (b + 1))
                wait_past(pe, logits_ready, score_no(b, h, qt) - 2)
                toks = slice(qt * P, (qt + 1) * P)
                nc.tensor.matmul(ps_s[qt % 2][:, :], lhsT=q_hl[:, h, toks], rhs=k_hl[:, h, :],
                                 start=True, stop=False)
                nc.tensor.matmul(ps_s[qt % 2][:, :], lhsT=q_lh[:, h, toks], rhs=k_hl[:, h, :],
                                 start=False, stop=True).then_inc(scores_ready, 1)

            def transpose_probs(b, h, pair):
                pe.wait_ge(probs_ready, score_no(b, h, 2 * pair + 1))
                wait_past(pe, pT_lo_done, pair_no(b, h, pair) - 2)
                for j in range(2):
                    for kt in range(TT):
                        last = nc.tensor.transpose(ps_t[pair][:, j, kt * P:(kt + 1) * P],
                                                   probs[:, ring(h, 2 * pair + j), kt * P:(kt + 1) * P],
                                                   ident[:, :])
                last.then_inc(transposed, 1)

            def attend(b, h):
                if h == 0:
                    pe.wait_ge(v_lo_done, TT * b + TT)
                pe.wait_ge(pT_lo_done, pair_no(b, h, 1))
                out = ps_g[shared_bank(f"pv{h}")][0:V_COLS, :]
                for kt in range(TT):
                    v_head = v_s[:, kt, h, :]
                    for part, pT in enumerate((pT_hi, pT_lo)):
                        last = nc.tensor.matmul(out, lhsT=v_head, rhs=pT[:, :, kt, :],
                                                start=(kt == 0 and part == 0), stop=(kt == TT - 1 and part == 1))
                last.then_inc(pv_ready, 1)

            def project_out(b, t):
                toks = slice(t * P, (t + 1) * P)
                three_passes(ps_g[shared_bank(f"wo{t}")][:, 0:D],
                             [((ctx_hi[:, k, toks], ctx_lo[:, k, toks]),
                               (w_hi["o"][:, k, :], w_lo["o"][:, k, :])) for k in range(KT)], wo_ready)

            def batch(b, first=False, last=False):
                for p in range(PAIRS):
                    if not (last and p + AHEAD >= PAIRS):
                        nb, nh, pair = pair_at(b, p + AHEAD)
                        scores(nb, nh, 2 * pair)
                        scores(nb, nh, 2 * pair + 1)
                    if p % 2 == 0 and not (first and p == 0):
                        of, h = (b, p // 2 - 1) if p else (b - 1, H - 1)
                        wait_for_bank(f"pv{h}", b)
                        attend(of, h)
                    transpose_probs(b, p // 2, p % 2)
                    for step, kind, t in steps_of(p, b, ("v", "q", "k", "wo")):
                        wait_for_bank(step, b)
                        if kind == "v":
                            project_v(b, t)
                        elif kind == "wo":
                            if t == 0:
                                pe.wait_ge(ctx_split, KT * b)
                            project_out(b - 1, t)
                        else:
                            of = batch_of(step, b)
                            if t == 0 and kind == "q":
                                pe.wait_ge(xT_split, KT * (of + 1))
                            project(of, kind, t, shared_bank(step))

            pe.wait_ge(consts_ready, 4)
            pe.wait_ge(xT_split, KT)
            for i, step in enumerate(PROLOGUE_USES):
                pe.wait_ge(w_ready[step[0]], 1)
                if i >= 2:
                    pe.wait_ge(proj_lo, i - 1)
                project(0, step[0], int(step[1]), shared_bank(step, prologue=True))
            for p in range(AHEAD):
                for qt in range(2 * (p % 2), 2 * (p % 2) + 2):
                    scores(0, p // 2, qt)
            pe.wait_ge(w_ready["v"], 1)
            batch(0, first=True)
            pe.wait_ge(w_ready["o"], 1)
            with pe.Fori(1, LAST) as b:
                batch(b)
            batch(LAST, last=True)
            wait_for_bank("pv7", B)
            attend(LAST, H - 1)
            pe.wait_ge(ctx_split, KT * B)
            for t in range(TT):
                bank = shared_bank(f"wo{t}")
                pe.wait_ge(ctx_staged, H * B)
                for earlier in range(t):
                    if shared_bank(f"wo{earlier}") == bank:
                        pe.wait_ge(resid_ready, TT * LAST + earlier + 1)
                project_out(LAST, t)


def feed_forward_phase(nc, x, w1, b1T, w2, b2, alpha2, gamma2, x1_dram, out):
    ctx = ExitStack()
    with ctx:
        def sb(name, shape, dt=FP32):
            return ctx.enter_context(nc.sbuf_tensor(name, shape, dt))

        def pb(name, shape):
            return ctx.enter_context(nc.psum_tensor(name, shape, FP32))

        def sem(name):
            return ctx.enter_context(nc.semaphore(name))

        BUFS = 3
        w1_hi = sb("w1_hi", [P, KT, F], FP32R)
        w1_lo = sb("w1_lo", [P, KT, F], FP32R)
        w2_hi = sb("w2_hi", [P, JT, D], FP32R)
        w2_lo = sb("w2_lo", [P, JT, D], FP32R)
        w1_raw = sb("w1_raw", [P, KT, F])
        w2_raw = sb("w2_raw", [P, JT, D])
        x1_rows = sb("x1_rows", [P, TT, D])
        x1T_hi = sb("x1T_hi", [P, KT, N], FP32R)
        x1T_lo = sb("x1T_lo", [P, KT, N], FP32R)
        hidden = sb("hidden", [P, BUFS, N])
        h_hi = sb("h_hi", [P, JT, N], FP32R)
        h_lo = sb("h_lo", [P, JT, N], FP32R)
        y = sb("y", [P, TT, D])
        z = sb("z", [P, TT, D])
        b1_c = sb("b1_c", [P, JT])
        b2_b = sb("b2_b", [P, D])
        alpha_b = sb("alpha2_b", [P, D])
        gamma_b = sb("gamma2_b", [P, D])
        ident = sb("ident2", [P, P])
        squares = sb("squares2", [P, D])
        sum_sq = sb("sum_sq2", [P, TT])
        mean_sq = sb("mean_sq2", [P, TT])
        rms = sb("rms2", [P, TT])
        stats = sb("stats", [P, TT, 6])
        mean_var = sb("mean_var", [P, TT, 2])
        var_eps = sb("var_eps", [P, TT])
        inv_std = sb("inv_std", [P, TT])
        minus_half = sb("minus_half2", [P, TT])

        ps_h = [pb(f"ps_h{i}", [P, N]) for i in range(BUFS)]
        ps_x = [pb(f"ps_x{i}", [P, N]) for i in range(KT)]
        ps_y = [pb(f"ps_y{i}", [P, N]) for i in range(2)]

        w1_loaded = sem("w1_loaded")
        w2_loaded = sem("w2_loaded")
        consts_loaded = sem("consts2_loaded")
        consts_ready = sem("consts2_ready")
        x1_loaded = sem("x1_loaded")
        rows_loaded = sem("rows2_loaded")
        w_step = sem("w12_step")
        w1_ready = sem("w1_ready")
        w2_ready = sem("w2_ready")
        x1_transposed = sem("x1_transposed")
        x1T_hi_done = sem("x1T_hi_done")
        x1T_lo_done = sem("x1T_lo_done")
        up_ready = sem("up_ready")
        hidden_ready = sem("hidden_ready")
        h_hi_done = sem("h_hi_done")
        h_lo_done = sem("h_lo_done")
        down_ready = sem("down_ready")
        xb2_ready = sem("xb2_ready")
        xg_ready = sem("xg_ready")
        resid_ready = sem("resid2_ready")
        squared = sem("squared2")
        mean_ready = sem("mean2_ready")
        rms_ready = sem("rms_ready")
        normed = sem("normed")
        summed = sem("summed")
        stats_done = sem("stats_done")
        aggregated = sem("aggregated")
        var_ready = sem("var_ready")
        inv_std_ready = sem("inv_std_ready")
        out_ready = sem("out_ready")
        out_stored = sem("out_stored")

        block = ctx.enter_context(nc.Block())

        @block.sync
        def _(sp):
            def rows(ap):
                return ap.rearrange("(t p) d -> p t d", p=P)

            def batch(b, first=False, last=False):
                wait_past(sp, out_stored, DMA * TT * b)
                sp.dma_start(z[:, :, :], rows(x[b])).then_inc(rows_loaded, DMA)
                if not last:
                    wait_apart(sp, x1_transposed, KT * (b + 1), rows_loaded)
                    wait_apart(sp, xb2_ready, TT * (b + 1), rows_loaded)
                    sp.dma_start(x1_rows[:, :, :], rows(x1_dram[b + 1])).then_inc(x1_loaded, DMA)
                for t in range(TT):
                    store(b, t)

            def store(b, t):
                sp.wait_ge(out_ready, TT * b + t + 1)
                sp.dma_start(out[b, t * P:(t + 1) * P, :], z[:, t, :]).then_inc(out_stored, DMA)

            sp.dma_start(x1_rows[:, :, :], rows(x1_dram[0])).then_inc(x1_loaded, DMA)
            for k in range(KT):
                sp.dma_start(w1_raw[:, k, :], w1[k * P:(k + 1) * P, :]).then_inc(w1_loaded, DMA)
            sp.dma_start(b1_c[:, :], b1T).then_inc(consts_loaded, DMA)
            sp.dma_start(w2_raw[:, :, :], w2.rearrange("(j p) d -> p j d", p=P)).then_inc(w2_loaded, DMA)
            sp.dma_start(b2_b[:, :], b2.partition_broadcast(P)).then_inc(consts_loaded, DMA)
            sp.dma_start(alpha_b[:, :], alpha2.partition_broadcast(P)).then_inc(consts_loaded, DMA)
            sp.dma_start(gamma_b[:, :], gamma2.partition_broadcast(P)).then_inc(consts_loaded, DMA)
            batch(0, first=True)
            with sp.Fori(1, LAST) as b:
                batch(b)
            batch(LAST, last=True)
            sp.wait_ge(out_stored, DMA * TT * B)

        @block.gpsimd
        def _(pool):
            def inverse_rms(b, t):
                wait_apart(pool, squared, TT * b + t + 1, consts_ready)
                pool.tensor_scalar(mean_sq[:, t:t + 1], sum_sq[:, t:t + 1], 1.0 / D, EPS_RMS,
                                   ALU.mult, ALU.add).then_inc(mean_ready, 1)
                pool.wait_ge(mean_ready, TT * b + t + 1)
                pool.tensor_tensor(rms[:, t:t + 1], mean_sq[:, t:t + 1], minus_half[:, t:t + 1], ALU.pow)\
                    .then_inc(rms_ready, 1)

            def inverse_std(b, t):
                wait_apart(pool, aggregated, TT * b + t + 1, consts_ready)
                pool.tensor_scalar(var_eps[:, t:t + 1], mean_var[:, t, 1:2], EPS_LN, None, ALU.add)\
                    .then_inc(var_ready, 1)
                pool.wait_ge(var_ready, TT * b + t + 1)
                pool.tensor_tensor(inv_std[:, t:t + 1], var_eps[:, t:t + 1], minus_half[:, t:t + 1], ALU.pow)\
                    .then_inc(inv_std_ready, 1)

            def batch(b, first=False, last=False):
                if not first:
                    inverse_std(b - 1, TT - 1)
                pool.wait_ge(x1_loaded, DMA * (b + 1))
                wait_past(pool, summed, TT * b)
                for t in range(TT):
                    pool.tensor_tensor(y[:, t, :], x1_rows[:, t, :], b2_b[:, :], ALU.add)\
                        .then_inc(xb2_ready, 1)
                pool.wait_ge(rows_loaded, DMA * (b + 1))
                for t in range(TT):
                    pool.tensor_tensor(z[:, t, :], z[:, t, :], gamma_b[:, :], ALU.add).then_inc(xg_ready, 1)
                for t in range(TT):
                    inverse_rms(b, t)
                    if t > 0:
                        inverse_std(b, t - 1)

            pool.memset(minus_half[:, :], -0.5).then_inc(consts_ready, 1)
            pool.memset(ident[:, :], 0.0).then_inc(consts_ready, 1)
            pool.wait_ge(consts_ready, 2)
            pool.affine_select(out=ident[:, :], in_=ident[:, :], compare_op=ALU.not_equal, fill=1.0,
                               base=0, pattern=[[-1, P]], channel_multiplier=1).then_inc(consts_ready, 1)
            pool.wait_ge(w2_loaded, DMA)
            pool.tensor_copy(w2_hi[:, :, :], w2_raw[:, :, :]).then_inc(w2_ready, 1)
            pool.wait_ge(w2_ready, 1)
            pool.tensor_tensor(w2_lo[:, :, :], w2_raw[:, :, :], w2_hi[:, :, :].bitcast(FP32), ALU.subtract)\
                .then_inc(w2_ready, 1)
            pool.wait_ge(consts_loaded, 4 * DMA)
            batch(0, first=True)
            with pool.Fori(1, LAST) as b:
                batch(b)
            batch(LAST, last=True)
            inverse_std(LAST, TT - 1)

        @block.scalar
        def _(act):
            def x1T_high(b, k):
                act.wait_ge(x1_transposed, KT * b + k + 1)
                wait_past(act, up_ready, JT * b)
                nc.scalar.activation(x1T_hi[:, k, :], ps_x[k][:, :], ACT.Copy).then_inc(x1T_hi_done, 1)

            def batch(b, last=False):
                for j in range(JT):
                    act.wait_ge(up_ready, JT * b + j + 1)
                    wait_past(act, h_lo_done, JT * b + j + 1 - BUFS)
                    nc.scalar.activation(hidden[:, j % BUFS, :], ps_h[j % BUFS][:, :], ACT.Silu,
                                         bias=b1_c[:, j:j + 1]).then_inc(hidden_ready, 1)
                if not last:
                    for k in range(KT):
                        x1T_high(b + 1, k)
                for t in range(TT):
                    act.wait_ge(resid_ready, TT * b + t + 1)
                    wait_past(act, squared, TT * b + t)
                    nc.scalar.activation(squares[:, :], y[:, t, :], ACT.Square,
                                         accum_out=sum_sq[:, t:t + 1]).then_inc(squared, 1)

            for k in range(KT):
                x1T_high(0, k)
            act.wait_ge(consts_loaded, 4 * DMA)
            batch(0)
            with act.Fori(1, LAST) as b:
                batch(b)
            batch(LAST, last=True)

        @block.vector
        def _(dve):
            def x1T_low(b, k):
                dve.wait_ge(x1T_hi_done, KT * b + k + 1)
                nc.vector.tensor_tensor(x1T_lo[:, k, :], ps_x[k][:, :], x1T_hi[:, k, :].bitcast(FP32),
                                        ALU.subtract).then_inc(x1T_lo_done, 1)

            def residual(b, t):
                dve.wait_ge(down_ready, TT * b + t + 1)
                dve.wait_ge(xb2_ready, TT * b + t + 1)
                nc.vector.tensor_tensor(y[:, t, :], ps_y[t % 2][:, 0:D], y[:, t, :], ALU.add)\
                    .then_inc(resid_ready, 1)

            def second_sum(b, t):
                dve.wait_ge(rms_ready, TT * b + t + 1)
                nc.vector.scalar_tensor_tensor(out=y[:, t, :], in0=y[:, t, :], scalar=rms[:, t:t + 1],
                                               in1=alpha_b[:, :], op0=ALU.mult, op1=ALU.mult).then_inc(normed, 1)
                dve.wait_ge(xg_ready, TT * b + t + 1)
                dve.wait_ge(normed, TT * b + t + 1)
                nc.vector.tensor_tensor(z[:, t, :], y[:, t, :], z[:, t, :], ALU.add).then_inc(summed, 1)
                dve.wait_ge(summed, TT * b + t + 1)
                nc.vector.bn_stats(stats[:, t, :], z[:, t, :]).then_inc(stats_done, 1)
                wait_apart(dve, stats_done, TT * b + t + 1, consts_loaded)
                nc.vector.bn_aggr(mean_var[:, t, :], stats[:, t, :]).then_inc(aggregated, 1)

            def finish(b, t):
                dve.wait_ge(inv_std_ready, TT * b + t + 1)
                nc.vector.tensor_scalar(z[:, t, :], z[:, t, :], mean_var[:, t, 0:1], inv_std[:, t:t + 1],
                                        ALU.subtract, ALU.mult).then_inc(out_ready, 1)

            def batch(b, first=False, last=False):
                for j in range(JT):
                    if j == 0:
                        wait_past(dve, down_ready, TT * b)
                    dve.wait_ge(hidden_ready, JT * b + j + 1)
                    nc.vector.tensor_copy(h_hi[:, j, :], hidden[:, j % BUFS, :]).then_inc(h_hi_done, 1)
                    dve.wait_ge(h_hi_done, JT * b + j + 1)
                    nc.vector.tensor_tensor(h_lo[:, j, :], hidden[:, j % BUFS, :], h_hi[:, j, :].bitcast(FP32),
                                            ALU.subtract).then_inc(h_lo_done, 1)
                    if j == 1 and not first:
                        second_sum(b - 1, TT - 1)
                        finish(b - 1, TT - 2)
                    if j == 3 and not first:
                        finish(b - 1, TT - 1)
                if not last:
                    for k in range(KT):
                        x1T_low(b + 1, k)
                for t in range(TT):
                    residual(b, t)
                    if t >= 1:
                        second_sum(b, t - 1)
                    if t >= 2:
                        finish(b, t - 2)

            for k in range(KT):
                dve.wait_ge(w1_loaded, KT * DMA)
                nc.vector.tensor_copy(w1_hi[:, k, :], w1_raw[:, k, :]).then_inc(w_step, 1)
                dve.wait_ge(w_step, k + 1)
                nc.vector.tensor_tensor(w1_lo[:, k, :], w1_raw[:, k, :], w1_hi[:, k, :].bitcast(FP32),
                                        ALU.subtract).then_inc(w1_ready, 1)
            dve.wait_ge(consts_loaded, 4 * DMA)
            for k in range(KT):
                x1T_low(0, k)
            batch(0, first=True)
            with dve.Fori(1, LAST) as b:
                batch(b)
            batch(LAST, last=True)
            second_sum(LAST, TT - 1)
            finish(LAST, TT - 2)
            finish(LAST, TT - 1)

        @block.tensor
        def _(pe):
            def three_passes(out_ps, pairs, done):
                n = 0
                for (a_hi, a_lo), (b_hi, b_lo) in pairs:
                    for lhsT, rhs in ((a_hi, b_hi), (a_hi, b_lo), (a_lo, b_hi)):
                        last = nc.tensor.matmul(out_ps, lhsT=lhsT, rhs=rhs, start=(n == 0),
                                                stop=(n == 3 * len(pairs) - 1))
                        n += 1
                last.then_inc(done, 1)

            def transpose_x1(b, k):
                wait_past(pe, x1T_lo_done, KT * b + k + 1 - KT)
                for t in range(TT):
                    last = nc.tensor.transpose(ps_x[k][:, t * P:(t + 1) * P], x1_rows[:, t, k * P:(k + 1) * P],
                                               ident[:, :])
                last.then_inc(x1_transposed, 1)

            def batch(b, first=False, last=False):
                pe.wait_ge(x1T_lo_done, KT * (b + 1))
                for j in range(JT):
                    wait_past(pe, hidden_ready, JT * b + j + 1 - BUFS)
                    cols = slice(j * P, (j + 1) * P)
                    three_passes(ps_h[j % BUFS][:, :],
                                 [((w1_hi[:, k, cols], w1_lo[:, k, cols]), (x1T_hi[:, k, :], x1T_lo[:, k, :]))
                                  for k in range(KT)], up_ready)
                if not last:
                    pe.wait_ge(x1_loaded, DMA * (b + 2))
                    for k in range(KT):
                        transpose_x1(b + 1, k)
                if first:
                    pe.wait_ge(w2_ready, 2)
                for t in range(TT):
                    wait_past(pe, resid_ready, TT * b + t + 1 - 2)
                    toks = slice(t * P, (t + 1) * P)
                    n = 0
                    for j in range(JT):
                        if t == 0:
                            pe.wait_ge(h_lo_done, JT * b + j + 1)
                        for lhsT, rhs in ((h_hi[:, j, toks], w2_hi[:, j, :]), (h_hi[:, j, toks], w2_lo[:, j, :]),
                                          (h_lo[:, j, toks], w2_hi[:, j, :])):
                            end = nc.tensor.matmul(ps_y[t % 2][:, 0:D], lhsT=lhsT, rhs=rhs, start=(n == 0),
                                                   stop=(n == 3 * JT - 1))
                            n += 1
                    end.then_inc(down_ready, 1)

            pe.wait_ge(consts_ready, 3)
            pe.wait_ge(x1_loaded, DMA)
            for k in range(KT):
                transpose_x1(0, k)
            pe.wait_ge(w1_ready, KT)
            batch(0, first=True)
            with pe.Fori(1, LAST) as b:
                batch(b)
            batch(LAST, last=True)


def transformer_layer(nc, x, xT, adj, wq, bqT, wk, bkT, wv, bv, wo, bo, w1, b1T, w2, b2,
                      alpha1, gamma1, alpha2, gamma2, out):
    x1_dram = nc.dram_tensor("x1_rows_dram", (B, N, D), FP32, kind="Internal").ap()
    attention_phase(nc, x, xT, adj, wq, bqT, wk, bkT, wv, bv, wo, bo, alpha1, gamma1, x1_dram)
    feed_forward_phase(nc, x, w1, b1T, w2, b2, alpha2, gamma2, x1_dram, out)


def kernel(x, adj, **layer):
    import numpy as _np
    import concourse.bacc as _bacc
    from concourse.bass_utils import run_bass_kernel_spmd as _run

    w = {name.removeprefix("L0_gnn_"): _np.asarray(a) for name, a in layer.items()}
    x = _np.asarray(x)

    def per_partition(v, tiles):
        return v.reshape(tiles, -1).T

    ins = [("x", x), ("xT", x.transpose(0, 2, 1)), ("adj", _np.asarray(adj)),
           ("wq", w["wq"]), ("bqT", per_partition(w["bq"], KT)),
           ("wk", w["wk"]), ("bkT", per_partition(w["bk"], KT)),
           ("wv", w["wv"]), ("bv", per_partition(w["bv"], H)),
           ("wo", w["wo"]), ("bo", w["bo"]), ("w1", w["w1"]), ("b1T", per_partition(w["b1"], JT)),
           ("w2", w["w2"]), ("b2", w["b2"]), ("alpha1", w["alpha1"]), ("gamma1", w["gamma1"]),
           ("alpha2", w["alpha2"]), ("gamma2", w["gamma2"])]
    nc = _bacc.Bacc("TRN2", target_bir_lowering=False, num_devices=1)
    arrays, args = {}, []
    for name, a in ins:
        arrays[f"in_{name}"] = _np.ascontiguousarray(a)
        args.append(nc.dram_tensor(f"in_{name}", a.shape, mybir.dt.from_np(a.dtype), kind="ExternalInput").ap())
    args.append(nc.dram_tensor("out_0", (B, N, D), FP32, kind="ExternalOutput").ap())
    transformer_layer(nc, *args)
    r = _run(nc, [arrays], core_ids=[0])
    return r.results[0]["out_0"]
```

```python
from contextlib import ExitStack

import concourse.bass as bass
from concourse import mybir

FP32 = mybir.dt.float32
FP32R = mybir.dt.float32r
ALU = mybir.AluOpType
ACT = mybir.ActivationFunctionType

P = 128
B, N, D = 16, 512, 384
H = 8
DH = D // H
F = 1536
TT = N // P
KT = D // P
JT = F // P
LAST = B - 1
EPS_RMS = 1e-6
EPS_LN = 1e-5
BIG = 3.0e38
DMA = 16


def pieces_of_head(h):
    out, f, end = [], h * DH, (h + 1) * DH
    while f < end:
        t = f // P
        n = min(end, (t + 1) * P) - f
        out.append((t, f - t * P, f - h * DH, n))
        f += n
    return out


def heads_of_tile(t):
    return [h for h in range(H) if any(p[0] == t for p in pieces_of_head(h))]


LO = 64
V_COLS = LO + DH

STACK_DMAS = [2 * len(heads_of_tile(t)) for t in range(KT)]
PAIRS = 2 * H
AHEAD = 3
SIDE = {0: ["k2"], 1: ["v0", "v1"], 2: ["v2", "v3"], 6: ["q0"], 8: ["k0"], 10: ["q1"], 12: ["k1"], 14: ["q2"]}
XT_AT = (2, 3, 4)
PROLOGUE_USES = ["q0", "k0", "q1", "k1", "q2"]
PARTS_HI = {"q": (0, 2), "k": (0,)}
PROJECTIONS = [f"{kind}{t}" for t in range(KT) for kind in "qk"]
SHARED_USES = [s for p in range(PAIRS) for s in ([f"pv{(p // 2 - 1) % H}"] if p % 2 else []) + SIDE.get(p, [])]
assert len(SHARED_USES) % 2 == 0


def left_out(step, b):
    if not isinstance(b, int):
        return False
    return b == 0 and step == "pv7" or b == LAST and step in PROLOGUE_USES


def batch_of(step, b):
    if step == "pv7":
        return b - 1
    return b + 1 if step in PROLOGUE_USES else b


def shared_bank(step, prologue=False):
    return (PROLOGUE_USES if prologue else SHARED_USES).index(step) % 2


def use_before(step, b):
    at = SHARED_USES.index(step)
    for s in SHARED_USES[at % 2:at:2][::-1]:
        if not left_out(s, b):
            return s, batch_of(s, b)
    if isinstance(b, int) and b == 0:
        return PROLOGUE_USES[at % 2::2][-1], 0
    s = [s for s in SHARED_USES[at % 2::2] if not left_out(s, b - 1)][-1]
    return s, batch_of(s, b - 1)


def steps_of(p, b, kinds):
    return [(s, s[:-1], int(s[-1])) for s in SIDE.get(p, []) if s[:-1] in kinds and not left_out(s, b)]


def pair_at(b, p):
    return b + p // PAIRS, p % PAIRS // 2, p % 2


def pairs_of(b, p):
    if isinstance(b, int) and not 0 <= b + p // PAIRS < B:
        return []
    return [pair_at(b, p)]


def wait_past(eng, sem, value):
    if isinstance(value, int) and value <= 0:
        return
    eng.wait_ge(sem, value)


def wait_apart(eng, sem, value, passed):
    if isinstance(value, int):
        wait_past(eng, sem, value)
    else:
        eng.compute_val(value)
        eng.wait_ge(passed, 1)
        eng.wait_ge(sem, value)


class Shared:

    def __init__(self, nc, stack):
        def sb(name, shape, dt=FP32):
            return stack.enter_context(nc.sbuf_tensor(name, shape, dt))

        self.wo_hi = sb("wo_hi", [P, KT, D], FP32R)
        self.wo_lo = sb("wo_lo", [P, KT, D], FP32R)
        self.ctx_a = sb("ctx_a", [P, KT, N])
        self.ctx_b = sb("ctx_b", [P, KT, N])
        self.ctx_loaded = stack.enter_context(nc.semaphore("ctx_loaded"))
        self.ctx_summed = stack.enter_context(nc.semaphore("ctx_summed"))

    def load_context(self, sp, ctx_dram, b):
        for part, buf in enumerate((self.ctx_a, self.ctx_b)):
            sp.dma_start(buf[:, :, :], ctx_dram[b, part].rearrange("(k p) n -> p k n", p=P))\
              .then_inc(self.ctx_loaded, DMA)

    def sum_context(self, pool, b):
        pool.wait_ge(self.ctx_loaded, 2 * DMA * (b + 1))
        for k in range(KT):
            pool.tensor_tensor(self.ctx_a[:, k, :], self.ctx_a[:, k, :], self.ctx_b[:, k, :], ALU.add)\
                .then_inc(self.ctx_summed, 1)


def attention_phase(nc, shared, xT, adj, wq, bqT, wk, bkT, wv, bv, wo, ctx_dram):
    ctx = ExitStack()
    with ctx:
        def sb(name, shape, dt=FP32):
            return ctx.enter_context(nc.sbuf_tensor(name, shape, dt))

        def pb(name, shape):
            return ctx.enter_context(nc.psum_tensor(name, shape, FP32))

        def sem(name):
            return ctx.enter_context(nc.semaphore(name))

        w_hi = {n: sb(f"w{n}_hi", [P, KT, D], FP32R) for n in "qkv"}
        w_lo = {n: sb(f"w{n}_lo", [P, KT, D], FP32R) for n in "qkv"}
        xT_raw = sb("xT_raw", [P, KT, N])
        xT_hi = sb("xT_hi", [P, KT, N], FP32R)
        xT_lo = sb("xT_lo", [P, KT, N], FP32R)
        stage = {"q": sb("stage_q", [P, 3, N], FP32R), "k": sb("stage_k", [P, 2, N], FP32R)}
        q_both = sb("q_both", [2 * DH, H, 2, N], FP32R)
        k_hl = sb("k_hl", [2 * DH, H, N], FP32R)
        v_s = sb("v_s", [P, TT, H, V_COLS], FP32R)
        adj_s = sb("adj_s", [P, TT, N])
        adj_first = sb("adj_first", [P, 2, N])
        probs = sb("probs", [P, 8, N])
        pT_hi = sb("pT_hi", [P, 2, TT, TT, P], FP32R)
        pT_lo = sb("pT_lo", [P, 2, TT, TT, P], FP32R)
        ctx_stage = sb("ctx_stage", [P, 2, N])
        bq_c = sb("bq_c", [P, KT])
        bk_c = sb("bk_c", [P, KT])
        bv_c = sb("bv_c", [P, H])
        ident = sb("ident", [P, P])
        row_max = sb("row_max", [P, 2 * TT])
        neg_max = sb("neg_max", [P, 2 * TT])
        row_sum = sb("row_sum", [P, 2 * TT])
        inv_sum = sb("inv_sum", [P, 2 * TT])
        ps_s = [pb(f"ps_s{i}", [P, N]) for i in range(2)]
        ps_t = [pb(f"ps_t{i}", [P, 2, N]) for i in range(2)]
        ps_g = [pb(f"ps_g{i}", [P, N]) for i in range(2)]

        w_loaded = {n: sem(f"w{n}_loaded") for n in "qkv"}
        consts_loaded = sem("consts_loaded")
        xT_loaded = sem("xT_loaded")
        adj_loaded = [sem(f"adj_loaded{i}") for i in range(2)]
        adj_first_loaded = sem("adj_first_loaded")
        zeroed = sem("zeroed")
        consts_ready = sem("consts_ready")
        w_step = sem("w_step")
        w_ready = {n: sem(f"w{n}_split") for n in "qkv"}
        xT_hi_done = sem("xT_hi_done")
        xT_split = sem("xT_split")
        proj_ready = sem("proj_ready")
        proj_hi = sem("proj_hi")
        proj_lo = sem("proj_lo")
        stacked = {n: [sem(f"{n}_stacked{t}") for t in range(KT)] for n in "qk"}
        v_ready = sem("v_ready")
        v_hi_done = sem("v_hi_done")
        v_lo_done = sem("v_lo_done")
        scores_ready = sem("scores_ready")
        logits_ready = sem("logits_ready")
        neg_max_ready = sem("neg_max_ready")
        exp_done = sem("exp_done")
        inv_done = sem("inv_done")
        probs_ready = [sem(f"probs_ready{i}") for i in range(2)]
        transposed = sem("transposed")
        pT_hi_done = sem("pT_hi_done")
        pT_lo_done = sem("pT_lo_done")
        pv_ready = sem("pv_ready")
        ctx_staged = sem("ctx_staged")
        ctx_stored = [sem(f"ctx_stored{i}") for i in range(2)]
        bq_scaled = sem("bq_scaled")
        wo_loaded = sem("wo_loaded")
        wo_hi_done = sem("wo_hi_done")
        wo_split = sem("wo_split")
        wo_raw = shared.ctx_a[:, :, 0:D]

        def score_no(b, h, qt):
            return H * TT * b + TT * h + qt + 1

        def ring(h, qt):
            return (TT * h + qt) % 8

        def pair_no(b, h, pair):
            return 2 * H * b + 2 * h + pair + 1

        def proj_at(kind, t):
            return PROJECTIONS.index(f"{kind}{t}")

        def proj_no(b, kind, t):
            return 2 * KT * b + proj_at(kind, t) + 1

        def proj_hi_no(b, kind, t, parts):
            return 3 * KT * b + sum(len(PARTS_HI[s[0]]) for s in PROJECTIONS[:proj_at(kind, t)]) + parts

        def context_at(b, p):
            return pairs_of(b, p - 2) if p % 2 else []

        block = ctx.enter_context(nc.Block())

        @block.sync
        def _(sp):
            def load_xT(b):
                sp.dma_start(xT_raw[:, :, :], xT[b].rearrange("(k p) n -> p k n", p=P)).then_inc(xT_loaded, DMA)

            def load_adj(tile, b, pair, loaded):
                rows = adj[b, 2 * pair * P:2 * (pair + 1) * P, :]
                sp.dma_start(tile, rows.rearrange("(t p) k -> p t k", p=P)).then_inc(loaded, DMA)

            def load_adj_pair(b, pair):
                wait_apart(sp, logits_ready, score_no(b - 1, H - 1, 2 * pair + 1), zeroed)
                load_adj(adj_s[:, 2 * pair:2 * pair + 2, :], b, pair, adj_loaded[pair])

            def stack_projection(b, kind, t, earlier):
                if not isinstance(earlier, int) or earlier >= 0:
                    wait_apart(sp, scores_ready, score_no(earlier, heads_of_tile(t)[-1], TT - 1), zeroed)
                wait_apart(sp, proj_lo, proj_no(b, kind, t), zeroed)
                sp.wait_ge(proj_hi, proj_hi_no(b, kind, t, len(PARTS_HI[kind])))
                for h in heads_of_tile(t):
                    for tile, src, dst, n in pieces_of_head(h):
                        if tile != t:
                            continue
                        for part, row in enumerate((dst, DH + dst)):
                            if kind == "q":
                                to = q_both[row:row + n, h, :, :]
                                part_of = stage[kind][src:src + n, part:part + 2, :]
                            else:
                                to, part_of = k_hl[row:row + n, h, :], stage[kind][src:src + n, part, :]
                            sp.dma_start(to.bitcast(FP32), part_of.bitcast(FP32)).then_inc(stacked[kind][t], DMA)

            def store_context(b, h):
                sp.wait_ge(ctx_staged, H * b + h + 1)
                for part, row in enumerate((0, LO)):
                    sp.dma_start(ctx_dram[b, part, h * DH:(h + 1) * DH, :],
                                 ctx_stage[row:row + DH, h % 2, :]).then_inc(ctx_stored[h % 2], DMA)

            def batch(b, last=False):
                for p in range(PAIRS):
                    if p == 0 and not last:
                        sp.wait_ge(xT_split, KT * (b + 1))
                        load_xT(b + 1)
                    if p == 1 and not last:
                        wait_apart(sp, logits_ready, score_no(b, 0, 1), zeroed)
                        load_adj(adj_first[:, :, :], b + 1, 0, adj_first_loaded)
                    if p == 1 and last:
                        sp.wait_ge(wo_split, 1)
                        for par in range(2):
                            sp.wait_ge(ctx_stored[par], 2 * DMA * H // 2)
                        shared.load_context(sp, ctx_dram, 0)
                    if p in (11, 12) and not last:
                        load_adj_pair(b + 1, p - 11)
                    for step, kind, t in steps_of(p - 1, b, "qk"):
                        of = batch_of(step, b)
                        stack_projection(of, kind, t, of - 1)
                    for of, h, _ in context_at(b, p):
                        store_context(of, h)

            wide = probs[:, :, :].rearrange("p a n -> p (a n)")
            for i, (n, w) in enumerate((("q", wq), ("k", wk), ("v", wv))):
                sp.dma_start(wide[:, i * KT * D:(i + 1) * KT * D].rearrange("p (k n) -> p k n", k=KT),
                             w.rearrange("(k p) n -> p k n", p=P)).then_inc(w_loaded[n], DMA)
                if n == "q":
                    load_xT(0)
                    sp.dma_start(bq_c[:, :], bqT).then_inc(consts_loaded, DMA)
                    sp.dma_start(bk_c[:, :], bkT).then_inc(consts_loaded, DMA)
            sp.wait_ge(zeroed, 1)
            sp.dma_start(bv_c[0:DH, :], bv).then_inc(consts_loaded, DMA)
            load_adj(adj_first[:, :, :], 0, 0, adj_first_loaded)
            load_adj(adj_s[:, 2:4, :], 0, 1, adj_loaded[1])
            load_adj(adj_s[:, 0:2, :], 0, 0, adj_loaded[0])
            sp.dma_start(wo_raw, wo.rearrange("(k p) d -> p k d", p=P)).then_inc(wo_loaded, DMA)
            for step in PROLOGUE_USES:
                stack_projection(0, step[0], int(step[1]), -1)
            batch(0)
            with sp.Fori(1, LAST) as b:
                batch(b)
            batch(LAST, last=True)
            store_context(LAST, H - 1)
            for par in range(2):
                sp.wait_ge(ctx_stored[par], 2 * DMA * B * H // 2)

        @block.gpsimd
        def _(pool):
            def xT_low(b, k):
                wait_apart(pool, xT_hi_done, KT * b + k + 1, consts_ready)
                pool.tensor_tensor(xT_lo[:, k, :], xT_raw[:, k, :], xT_hi[:, k, :].bitcast(FP32),
                                   ALU.subtract).then_inc(xT_split, 1)

            def normalise(b, h, pair):
                at = ring(h, 2 * pair + 1)
                wait_apart(pool, inv_done, pair_no(b, h, pair), consts_ready)
                pool.tensor_scalar(probs[:, at, :], probs[:, at, :], inv_sum[:, at:at + 1], None,
                                   ALU.mult).then_inc(probs_ready[1], 1)

            def batch(b, last=False):
                for p in range(PAIRS):
                    for pair in pairs_of(b, p + AHEAD - 1):
                        normalise(*pair)
                    if p in XT_AT and not last:
                        xT_low(b + 1, p - XT_AT[0])
                    if p == 6 and last:
                        shared.sum_context(pool, 0)

            pool.memset(bv_c[:, :], 0.0).then_inc(zeroed, 1)
            pool.memset(v_s[:, :, :, DH:LO].bitcast(FP32), 0.0).then_inc(consts_ready, 1)
            pool.memset(ident[:, :], 0.0).then_inc(consts_ready, 1)
            pool.wait_ge(consts_ready, 2)
            pool.affine_select(out=ident[:, :], in_=ident[:, :], compare_op=ALU.not_equal, fill=1.0,
                               base=0, pattern=[[-1, P]], channel_multiplier=1).then_inc(consts_ready, 1)
            for k in range(KT):
                xT_low(0, k)
            pool.wait_ge(wo_loaded, DMA)
            pool.tensor_copy(shared.wo_hi[:, :, :], wo_raw).then_inc(wo_hi_done, 1)
            pool.wait_ge(wo_hi_done, 1)
            pool.tensor_tensor(shared.wo_lo[:, :, :], wo_raw, shared.wo_hi[:, :, :].bitcast(FP32), ALU.subtract)\
                .then_inc(wo_split, 1)
            for p in range(AHEAD - 1):
                normalise(0, p // 2, p % 2)
            batch(0)
            with pool.Fori(1, LAST) as b:
                batch(b)
            batch(LAST, last=True)

        @block.scalar
        def _(act):
            def project_hi(b, kind, t, bank):
                act.wait_ge(proj_ready, proj_no(b, kind, t))
                if t > 0:
                    act.wait_ge(stacked[kind][t - 1], DMA * STACK_DMAS[t - 1] * (b + 1))
                else:
                    wait_past(act, stacked[kind][KT - 1], DMA * STACK_DMAS[KT - 1] * b)
                bias = bq_c if kind == "q" else bk_c
                nc.scalar.activation(stage[kind][:, 0, :], ps_g[bank][:, :], ACT.Identity,
                                     bias=bias[:, t:t + 1]).then_inc(proj_hi, 1)
                if kind == "q":
                    act.wait_ge(proj_hi, proj_hi_no(b, kind, t, 1))
                    nc.scalar.activation(stage[kind][:, 2, :], stage[kind][:, 0, :].bitcast(FP32), ACT.Copy)\
                      .then_inc(proj_hi, 1)

            def xT_high(b, k):
                act.wait_ge(xT_loaded, DMA * (b + 1))
                wait_past(act, v_ready, TT * b)
                nc.scalar.activation(xT_hi[:, k, :], xT_raw[:, k, :], ACT.Copy).then_inc(xT_hi_done, 1)

            def v_hi(b, kt):
                act.wait_ge(v_ready, TT * b + kt + 1)
                wait_past(act, pv_ready, H * b)
                nc.scalar.activation(v_s[:, kt, :, 0:DH],
                                     ps_g[shared_bank(f"v{kt}")][:, 0:D].rearrange("p (h d) -> p h d", h=H),
                                     ACT.Copy)\
                  .then_inc(v_hi_done, 1)

            def exponent(b, h, qt):
                at = ring(h, qt)
                act.wait_ge(neg_max_ready, pair_no(b, h, qt // 2))
                nc.scalar.activation(probs[:, at, :], probs[:, at, :], ACT.Exp,
                                     bias=neg_max[:, at:at + 1], accum_out=row_sum[:, at:at + 1])\
                  .then_inc(exp_done, 1)

            def pT_high(b, h, pair):
                act.wait_ge(transposed, pair_no(b, h, pair))
                wait_past(act, pv_ready, H * b + h - 1)
                nc.scalar.activation(pT_hi[:, h % 2, 2 * pair:2 * pair + 2, :, :],
                                     ps_t[pair][:, :, :].rearrange("p q (k i) -> p q k i", k=TT), ACT.Copy)\
                  .then_inc(pT_hi_done, 1)

            def stage_context(b, h):
                act.wait_ge(pv_ready, H * b + h + 1)
                wait_past(act, ctx_stored[h % 2], 2 * DMA * (H // 2 * b + h // 2))
                bank = shared_bank(f"pv{h}")
                nc.scalar.activation(ctx_stage[0:V_COLS, h % 2, :], ps_g[bank][0:V_COLS, :], ACT.Identity,
                                     bias=bv_c[0:V_COLS, h:h + 1]).then_inc(ctx_staged, 1)

            def batch(b, last=False):
                for p in range(PAIRS):
                    pT_high(b, p // 2, p % 2)
                    for of, h, pair in pairs_of(b, p + AHEAD):
                        exponent(of, h, 2 * pair)
                        exponent(of, h, 2 * pair + 1)
                    for of, h, _ in context_at(b, p):
                        stage_context(of, h)
                    for step, kind, t in steps_of(p, b, ("v", "q", "k")):
                        if kind == "v":
                            v_hi(b, t)
                        else:
                            project_hi(batch_of(step, b), kind, t, shared_bank(step))
                    if p in XT_AT and not last:
                        xT_high(b + 1, p - XT_AT[0])

            for k in range(KT):
                xT_high(0, k)
            act.wait_ge(consts_loaded, 3 * DMA)
            act.wait_ge(consts_ready, 3)
            act.wait_ge(bq_scaled, 1)
            def prologue_hi(step):
                project_hi(0, step[0], int(step[1]), shared_bank(step, prologue=True))

            for step in PROLOGUE_USES[:-1]:
                prologue_hi(step)
            for p in range(AHEAD):
                for qt in range(2 * (p % 2), 2 * (p % 2) + 2):
                    exponent(0, p // 2, qt)
            prologue_hi(PROLOGUE_USES[-1])
            batch(0)
            with act.Fori(1, LAST) as b:
                batch(b)
            batch(LAST, last=True)
            stage_context(LAST, H - 1)

        @block.vector
        def _(dve):
            def project_lo(b, kind, t, bank):
                dve.wait_ge(proj_hi, proj_hi_no(b, kind, t, 1))
                bias = bq_c if kind == "q" else bk_c
                nc.vector.scalar_tensor_tensor(out=stage[kind][:, 1, :], in0=ps_g[bank][:, :],
                                               scalar=bias[:, t:t + 1], in1=stage[kind][:, 0, :].bitcast(FP32),
                                               op0=ALU.add, op1=ALU.subtract).then_inc(proj_lo, 1)

            def v_lo(b, kt):
                dve.wait_ge(v_hi_done, TT * b + kt + 1)
                nc.vector.tensor_tensor(v_s[:, kt, :, LO:V_COLS],
                                        ps_g[shared_bank(f"v{kt}")][:, 0:D].rearrange("p (h d) -> p h d", h=H),
                                        v_s[:, kt, :, 0:DH].bitcast(FP32), ALU.subtract).then_inc(v_lo_done, 1)

            def logits(b, h, pair):
                for qt in (2 * pair, 2 * pair + 1):
                    at = ring(h, qt)
                    rows = adj_first[:, qt, :] if h == 0 and pair == 0 else adj_s[:, qt, :]
                    wait_apart(dve, scores_ready, score_no(b, h, qt), consts_loaded)
                    if h == 0 and pair == 0:
                        wait_apart(dve, adj_first_loaded, DMA * (b + 1), consts_loaded)
                    elif h == 0 or h == 1 and pair == 0:
                        wait_apart(dve, adj_loaded[pair], DMA * (b + 1), consts_loaded)
                    wait_apart(dve, transposed, pair_no(b, h, pair) - 4, consts_loaded)
                    nc.vector.tensor_tensor_reduce(out=probs[:, at, :], in0=ps_s[qt % 2][:, :],
                                                   in1=rows, scale=1.0, scalar=-BIG,
                                                   op0=ALU.add, op1=ALU.max,
                                                   accum_out=row_max[:, at:at + 1]).then_inc(logits_ready, 1)

            def negate_max(b, h, pair):
                at = ring(h, 2 * pair)
                dve.wait_ge(logits_ready, score_no(b, h, 2 * pair + 1))
                nc.vector.tensor_scalar(neg_max[:, at:at + 2], row_max[:, at:at + 2], -1.0, None, ALU.mult)\
                    .then_inc(neg_max_ready, 1)

            def invert_sum(b, h, pair):
                at = ring(h, 2 * pair)
                dve.wait_ge(exp_done, score_no(b, h, 2 * pair + 1))
                nc.vector.reciprocal(inv_sum[:, at:at + 2], row_sum[:, at:at + 2]).then_inc(inv_done, 1)

            def normalise(b, h, pair):
                at = ring(h, 2 * pair)
                dve.wait_ge(inv_done, pair_no(b, h, pair))
                nc.vector.tensor_scalar(probs[:, at, :], probs[:, at, :], inv_sum[:, at:at + 1], None,
                                        ALU.mult).then_inc(probs_ready[0], 1)

            def pT_low(b, h, pair):
                dve.wait_ge(pT_hi_done, pair_no(b, h, pair))
                s = slice(2 * pair, 2 * pair + 2)
                nc.vector.tensor_tensor(pT_lo[:, h % 2, s, :, :].rearrange("p q k i -> p (q k i)"),
                                        ps_t[pair][:, :, :].rearrange("p q n -> p (q n)"),
                                        pT_hi[:, h % 2, s, :, :].rearrange("p q k i -> p (q k i)").bitcast(FP32),
                                        ALU.subtract).then_inc(pT_lo_done, 1)

            def batch(b):
                for p in range(PAIRS):
                    for ahead in pairs_of(b, p + AHEAD):
                        logits(*ahead)
                    for pair in pairs_of(b, p + AHEAD - 1):
                        invert_sum(*pair)
                    for ahead in pairs_of(b, p + AHEAD):
                        negate_max(*ahead)
                    for step, kind, t in steps_of(p - 1, b, "qk"):
                        project_lo(batch_of(step, b), kind, t, shared_bank(step))
                    pT_low(b, p // 2, p % 2)
                    for pair in pairs_of(b, p + AHEAD - 1):
                        normalise(*pair)
                    for _, _, kt in steps_of(p, b, "v"):
                        v_lo(b, kt)

            wide = probs[:, :, :].rearrange("p a n -> p (a n)")
            steps = 0
            for i, n in enumerate("qkv"):
                w_raw = wide[:, i * KT * D:(i + 1) * KT * D]
                dve.wait_ge(w_loaded[n], DMA)
                if n == "q":
                    nc.vector.tensor_scalar(w_raw, w_raw, DH ** -0.5, None, ALU.mult).then_inc(w_step, 1)
                    steps += 1
                    dve.wait_ge(w_step, steps)
                hi, lo = (w[n][:, :, :].rearrange("p k n -> p (k n)") for w in (w_hi, w_lo))
                nc.vector.tensor_copy(hi, w_raw).then_inc(w_step, 1)
                steps += 1
                dve.wait_ge(w_step, steps)
                nc.vector.tensor_tensor(lo, w_raw, hi.bitcast(FP32), ALU.subtract).then_inc(w_ready[n], 1)
                if n == "k":
                    dve.wait_ge(consts_loaded, 3 * DMA)
                    nc.vector.tensor_scalar(bq_c[:, :], bq_c[:, :], DH ** -0.5, None, ALU.mult)\
                        .then_inc(bq_scaled, 1)
            dve.wait_ge(bq_scaled, 1)
            dve.wait_ge(w_ready["v"], 1)
            def prologue_lo(step):
                project_lo(0, step[0], int(step[1]), shared_bank(step, prologue=True))

            for step in PROLOGUE_USES[:-1]:
                prologue_lo(step)
            for p in range(AHEAD):
                logits(0, p // 2, p % 2)
                negate_max(0, p // 2, p % 2)
                if p > 0:
                    invert_sum(0, (p - 1) // 2, (p - 1) % 2)
                    normalise(0, (p - 1) // 2, (p - 1) % 2)
            prologue_lo(PROLOGUE_USES[-1])
            batch(0)
            with dve.Fori(1, LAST) as b:
                batch(b)
            batch(LAST)

        @block.tensor
        def _(pe):
            def wait_for_bank(step, b):
                user, of = use_before(step, b)
                kind, no = user[:-1], int(user[-1])
                if kind == "v":
                    pe.wait_ge(v_lo_done, TT * of + no + 1)
                elif kind == "pv":
                    pe.wait_ge(ctx_staged, H * of + no + 1)
                else:
                    pe.wait_ge(proj_lo, proj_no(of, kind, no))

            def three_passes(out, pairs, done):
                n = 0
                for (a_hi, a_lo), (b_hi, b_lo) in pairs:
                    for lhsT, rhs in ((a_hi, b_hi), (a_hi, b_lo), (a_lo, b_hi)):
                        last = nc.tensor.matmul(out, lhsT=lhsT, rhs=rhs, start=(n == 0),
                                                stop=(n == 3 * len(pairs) - 1))
                        n += 1
                last.then_inc(done, 1)

            def project(kind, t, bank):
                cols = slice(t * P, (t + 1) * P)
                three_passes(ps_g[bank][:, :],
                             [((w_hi[kind][:, k, cols], w_lo[kind][:, k, cols]),
                               (xT_hi[:, k, :], xT_lo[:, k, :])) for k in range(KT)], proj_ready)

            def project_v(kt):
                toks = slice(kt * P, (kt + 1) * P)
                three_passes(ps_g[shared_bank(f"v{kt}")][:, 0:D],
                             [((xT_hi[:, k, toks], xT_lo[:, k, toks]),
                               (w_hi["v"][:, k, :], w_lo["v"][:, k, :])) for k in range(KT)], v_ready)

            def scores(b, h, qt):
                if qt == 0:
                    for t, *_ in pieces_of_head(h):
                        pe.wait_ge(stacked["q"][t], DMA * STACK_DMAS[t] * (b + 1))
                        pe.wait_ge(stacked["k"][t], DMA * STACK_DMAS[t] * (b + 1))
                wait_past(pe, logits_ready, score_no(b, h, qt) - 2)
                toks = slice(qt * P, (qt + 1) * P)
                nc.tensor.matmul(ps_s[qt % 2][:, :], lhsT=q_both[:, h, 0, toks], rhs=k_hl[:, h, :],
                                 start=True, stop=False)
                nc.tensor.matmul(ps_s[qt % 2][:, :], lhsT=q_both[:, h, 1, toks], rhs=k_hl[:, h, :],
                                 start=False, stop=True).then_inc(scores_ready, 1)

            def transpose_probs(b, h, pair):
                for i in range(2):
                    pe.wait_ge(probs_ready[i], pair_no(b, h, pair))
                wait_past(pe, pT_lo_done, pair_no(b, h, pair) - 2)
                for j in range(2):
                    for kt in range(TT):
                        last = nc.tensor.transpose(ps_t[pair][:, j, kt * P:(kt + 1) * P],
                                                   probs[:, ring(h, 2 * pair + j), kt * P:(kt + 1) * P],
                                                   ident[:, :])
                last.then_inc(transposed, 1)

            def attend(b, h):
                if h == 0:
                    pe.wait_ge(v_lo_done, TT * b + TT)
                pe.wait_ge(pT_lo_done, pair_no(b, h, 1))
                out = ps_g[shared_bank(f"pv{h}")][0:V_COLS, :]
                for kt in range(TT):
                    v_head = v_s[:, kt, h, :]
                    for part, pT in enumerate((pT_hi[:, h % 2], pT_lo[:, h % 2])):
                        last = nc.tensor.matmul(out, lhsT=v_head, rhs=pT[:, :, kt, :],
                                                start=(kt == 0 and part == 0), stop=(kt == TT - 1 and part == 1))
                last.then_inc(pv_ready, 1)

            def batch(b):
                for p in range(PAIRS):
                    for of, h, pair in pairs_of(b, p + AHEAD):
                        scores(of, h, 2 * pair)
                        scores(of, h, 2 * pair + 1)
                    transpose_probs(b, p // 2, p % 2)
                    for of, h, _ in context_at(b, p):
                        wait_for_bank(f"pv{h}", b)
                        attend(of, h)
                    for step, kind, t in steps_of(p, b, ("v", "q", "k")):
                        wait_for_bank(step, b)
                        if kind == "v":
                            project_v(t)
                        else:
                            of = batch_of(step, b)
                            if t == 0 and kind == "q":
                                pe.wait_ge(xT_split, KT * (of + 1))
                            project(kind, t, shared_bank(step))

            pe.wait_ge(consts_ready, 3)
            pe.wait_ge(xT_split, KT)
            def prologue_project(i):
                step = PROLOGUE_USES[i]
                pe.wait_ge(w_ready[step[0]], 1)
                if i >= 2:
                    pe.wait_ge(proj_lo, i - 1)
                project(step[0], int(step[1]), shared_bank(step, prologue=True))

            for i in range(len(PROLOGUE_USES) - 1):
                prologue_project(i)
            for p in range(AHEAD):
                for qt in range(2 * (p % 2), 2 * (p % 2) + 2):
                    scores(0, p // 2, qt)
            prologue_project(len(PROLOGUE_USES) - 1)
            pe.wait_ge(w_ready["v"], 1)
            batch(0)
            with pe.Fori(1, LAST) as b:
                batch(b)
            batch(LAST)
            wait_for_bank("pv7", B)
            attend(LAST, H - 1)


def feed_forward_phase(nc, shared, x, ctx_dram, bo, w1, b1T, w2, b2, alpha1, gamma1, alpha2, gamma2, out):
    ctx = ExitStack()
    with ctx:
        def sb(name, shape, dt=FP32):
            return ctx.enter_context(nc.sbuf_tensor(name, shape, dt))

        def pb(name, shape):
            return ctx.enter_context(nc.psum_tensor(name, shape, FP32))

        def sem(name):
            return ctx.enter_context(nc.semaphore(name))

        BUFS = 3
        wo_hi, wo_lo, ctx_a = shared.wo_hi, shared.wo_lo, shared.ctx_a
        w1_hi = sb("w1_hi", [P, KT, F], FP32R)
        w1_lo = sb("w1_lo", [P, KT, F], FP32R)
        w2_hi = sb("w2_hi", [P, JT, D], FP32R)
        w2_lo = sb("w2_lo", [P, JT, D], FP32R)
        ctx_hi = sb("ctx_hi", [P, KT, N], FP32R)
        ctx_lo = sb("ctx_lo", [P, KT, N], FP32R)
        x1 = sb("x1", [P, TT, D])
        x1T_hi = sb("x1T_hi", [P, KT, N], FP32R)
        x1T_lo = sb("x1T_lo", [P, KT, N], FP32R)
        hidden = sb("hidden", [P, BUFS, N])
        h_hi = sb("h_hi", [P, JT, N], FP32R)
        h_lo = sb("h_lo", [P, JT, N], FP32R)
        y = sb("y", [P, TT, D])
        z = sb("z", [P, TT, D])
        squares = [sb(f"squares{i}", [P, D], mybir.dt.bfloat16) for i in range(2)]
        b1_c = sb("b1_c", [P, JT])
        bo_b = sb("bo_b", [P, D])
        b2_b = sb("b2_b", [P, D])
        alpha1_b = sb("alpha1_b", [P, D])
        gamma1_b = sb("gamma1_b", [P, D])
        alpha2_b = sb("alpha2_b", [P, D])
        gamma2_b = sb("gamma2_b", [P, D])
        ident = sb("ident2", [P, P])
        minus_half = sb("minus_half", [P, TT])
        sum_sq = [sb(f"sum_sq{i}", [P, TT]) for i in range(2)]
        mean_sq = [sb(f"mean_sq{i}", [P, TT]) for i in range(2)]
        rms = [sb(f"rms{i}", [P, TT]) for i in range(2)]
        stats = sb("stats", [P, TT, 6])
        mean_var = sb("mean_var", [P, TT, 2])
        var_eps = sb("var_eps", [P, TT])
        inv_std = sb("inv_std", [P, TT])

        ps_h = [pb(f"ps_h{i}", [P, N]) for i in range(BUFS)]
        ps_x = [pb(f"ps_x{i}", [P, N]) for i in range(KT)]
        ps_y = [pb(f"ps_y{i}", [P, N]) for i in range(2)]

        chunk_loaded = [sem(f"chunk_loaded{i}") for i in range(6)]
        chunk_hi = sem("chunk_hi")
        chunk_lo = sem("chunk_lo")
        consts_loaded = sem("consts2_loaded")
        consts_ready = sem("consts2_ready")
        ctx_summed = shared.ctx_summed
        ctx_hi_done = sem("ctx_hi_done")
        ctx_split = sem("ctx_split")
        x1_rows_loaded = sem("x1_rows_loaded")
        xbo_ready = sem("xbo_ready")
        wo_ready = sem("wo_ready")
        resid1_ready = sem("resid1_ready")
        squared1 = sem("squared1")
        mean1_ready = sem("mean1_ready")
        rms1_ready = sem("rms1_ready")
        scaled1 = sem("scaled1")
        x1_ready = sem("x1_ready")
        x1_transposed = sem("x1_transposed")
        x1T_hi_done = sem("x1T_hi_done")
        x1T_lo_done = sem("x1T_lo_done")
        up_ready = sem("up_ready")
        hidden_ready = sem("hidden_ready")
        first_consts_loaded = sem("first_consts_loaded")
        h_hi_done = sem("h_hi_done")
        h_lo_done = sem("h_lo_done")
        down_ready = sem("down_ready")
        z_rows_loaded = sem("z_rows_loaded")
        xb2_ready = sem("xb2_ready")
        xg_ready = sem("xg_ready")
        resid2_ready = sem("resid2_ready")
        squared2 = sem("squared2")
        mean2_ready = sem("mean2_ready")
        rms2_ready = sem("rms2_ready")
        scaled2 = sem("scaled2")
        summed = sem("summed")
        stats_done = sem("stats_done")
        aggregated = sem("aggregated")
        var_ready = sem("var_ready")
        inv_std_ready = sem("inv_std_ready")
        out_ready = sem("out_ready")
        out_stored = sem("out_stored")

        def flat(a):
            return a.rearrange("p a b -> p (a b)")

        JC = JT // 3
        CHUNKS = []
        for k, buf in enumerate((y, z, hidden)):
            CHUNKS.append((flat(buf[:, :, :]), w1[k * P:(k + 1) * P, :], w1_hi[:, k, :], w1_lo[:, k, :]))
        for j, buf in zip(range(0, JT, JC), (y, z, z)):
            CHUNKS.append((flat(buf[:, :, :]), w2[j * P:(j + JC) * P, :].rearrange("(j p) d -> p j d", p=P),
                           flat(w2_hi[:, j:j + JC, :]), flat(w2_lo[:, j:j + JC, :])))
        W1_CHUNKS = 3
        CHUNK_BEFORE = {3: 0, 4: 1, 5: 4}
        CHUNK_AT = {2: 3, 5: 4, 8: 5}

        CTX_AT = {3: 0, 4: 1, 5: 2}
        WO_AT = {8: 0, 9: 1, 10: 2, 11: 3}

        block = ctx.enter_context(nc.Block())

        @block.sync
        def _(sp):
            def rows(ap):
                return ap.rearrange("(t p) d -> p t d", p=P)

            def load_chunk(i):
                if i in CHUNK_BEFORE:
                    sp.wait_ge(chunk_lo, CHUNK_BEFORE[i] + 1)
                buf, src, _, _ = CHUNKS[i]
                if len(src.shape) == 3:
                    buf = buf.rearrange("p (a b) -> p a b", b=src.shape[2])
                sp.dma_start(buf, src).then_inc(chunk_loaded[i], DMA)

            def load_z_rows(b):
                sp.dma_start(z[:, :, :], rows(x[b])).then_inc(z_rows_loaded, DMA)

            def load_x1_rows(b):
                sp.dma_start(x1[:, :, :], rows(x[b])).then_inc(x1_rows_loaded, DMA)

            def store(b, t):
                sp.wait_ge(out_ready, TT * b + t + 1)
                sp.dma_start(out[b, t * P:(t + 1) * P, :], z[:, t, :]).then_inc(out_stored, DMA)

            def batch(b, first=False, last=False):
                if not last:
                    sp.wait_ge(ctx_split, KT * (b + 1))
                    shared.load_context(sp, ctx_dram, b + 1)
                if not first:
                    for t in (TT - 2, TT - 1):
                        store(b - 1, t)
                    wait_apart(sp, out_stored, DMA * TT * b, consts_loaded)
                    load_z_rows(b)
                if not last:
                    wait_apart(sp, xb2_ready, TT * (b + 1), consts_loaded)
                    wait_apart(sp, x1_transposed, KT * (b + 1), consts_loaded)
                    load_x1_rows(b + 1)
                if first:
                    load_chunk(5)
                    sp.wait_ge(chunk_lo, 6)
                    load_z_rows(b)
                for t in (0, 1):
                    store(b, t)

            load_x1_rows(0)
            load_chunk(0)
            for tile, vector in ((bo_b, bo), (alpha1_b, alpha1), (gamma1_b, gamma1)):
                sp.dma_start(tile[:, :], vector.partition_broadcast(P)).then_inc(first_consts_loaded, DMA)
            load_chunk(1)
            load_chunk(2)
            sp.dma_start(b1_c[:, :], b1T).then_inc(consts_loaded, DMA)
            for tile, vector in ((b2_b, b2), (alpha2_b, alpha2), (gamma2_b, gamma2)):
                sp.dma_start(tile[:, :], vector.partition_broadcast(P)).then_inc(consts_loaded, DMA)
            load_chunk(3)
            load_chunk(4)
            batch(0, first=True)
            with sp.Fori(1, LAST) as b:
                batch(b)
            batch(LAST, last=True)
            for t in (TT - 2, TT - 1):
                store(LAST, t)
            sp.wait_ge(out_stored, DMA * TT * B)

        @block.gpsimd
        def _(pool):
            def power(n, b, t, squared, mean_ready, done):
                wait_apart(pool, squared, TT * b + t + 1, consts_ready)
                pool.tensor_scalar(mean_sq[n][:, t:t + 1], sum_sq[n][:, t:t + 1], 1.0 / D, EPS_RMS,
                                   ALU.mult, ALU.add).then_inc(mean_ready, 1)
                pool.wait_ge(mean_ready, TT * b + t + 1)
                pool.tensor_tensor(rms[n][:, t:t + 1], mean_sq[n][:, t:t + 1], minus_half[:, t:t + 1], ALU.pow)\
                    .then_inc(done, 1)

            def inverse_std(b, t):
                wait_apart(pool, aggregated, TT * b + t + 1, consts_ready)
                pool.tensor_scalar(var_eps[:, t:t + 1], mean_var[:, t, 1:2], EPS_LN, None, ALU.add)\
                    .then_inc(var_ready, 1)
                pool.wait_ge(var_ready, TT * b + t + 1)
                pool.tensor_tensor(inv_std[:, t:t + 1], var_eps[:, t:t + 1], minus_half[:, t:t + 1], ALU.pow)\
                    .then_inc(inv_std_ready, 1)

            def add_bo(b):
                pool.wait_ge(x1_rows_loaded, DMA * (b + 1))
                for t in range(TT):
                    pool.tensor_tensor(x1[:, t, :], x1[:, t, :], bo_b[:, :], ALU.add).then_inc(xbo_ready, 1)

            def first_norm(b):
                def add_gamma(t):
                    pool.wait_ge(scaled1, TT * b + t + 1)
                    pool.tensor_tensor(x1[:, t, :], x1[:, t, :], gamma1_b[:, :], ALU.add).then_inc(x1_ready, 1)

                for t in range(TT):
                    power(0, b, t, squared1, mean1_ready, rms1_ready)
                    if t > 0:
                        add_gamma(t - 1)
                add_gamma(TT - 1)

            def batch(b, first=False, last=False):
                if not first:
                    inverse_std(b - 1, TT - 1)
                if not last:
                    shared.sum_context(pool, b + 1)
                if first:
                    pool.wait_ge(chunk_lo, W1_CHUNKS + 1)
                else:
                    pool.wait_ge(summed, TT * b)
                for t in range(TT):
                    pool.tensor_tensor(y[:, t, :], x1[:, t, :], b2_b[:, :], ALU.add).then_inc(xb2_ready, 1)
                if not last:
                    add_bo(b + 1)
                pool.wait_ge(z_rows_loaded, DMA * (b + 1))
                for t in range(TT):
                    pool.tensor_tensor(z[:, t, :], z[:, t, :], gamma2_b[:, :], ALU.add).then_inc(xg_ready, 1)
                if not last:
                    first_norm(b + 1)
                for t in range(TT):
                    power(1, b, t, squared2, mean2_ready, rms2_ready)
                    if t > 0:
                        inverse_std(b, t - 1)

            pool.memset(minus_half[:, :], -0.5).then_inc(consts_ready, 1)
            pool.memset(ident[:, :], 0.0).then_inc(consts_ready, 1)
            pool.wait_ge(consts_ready, 2)
            pool.affine_select(out=ident[:, :], in_=ident[:, :], compare_op=ALU.not_equal, fill=1.0,
                               base=0, pattern=[[-1, P]], channel_multiplier=1).then_inc(consts_ready, 1)
            pool.wait_ge(first_consts_loaded, 3 * DMA)
            add_bo(0)
            first_norm(0)
            pool.wait_ge(consts_loaded, 4 * DMA)
            batch(0, first=True)
            with pool.Fori(1, LAST) as b:
                batch(b)
            batch(LAST, last=True)
            inverse_std(LAST, TT - 1)

        @block.scalar
        def _(act):
            def split_chunk(i):
                act.wait_ge(chunk_loaded[i], DMA)
                nc.scalar.activation(CHUNKS[i][2], CHUNKS[i][0], ACT.Copy).then_inc(chunk_hi, 1)

            def context_high(b, k):
                act.wait_ge(ctx_summed, KT * b + k + 1)
                wait_past(act, wo_ready, TT * b)
                nc.scalar.activation(ctx_hi[:, k, :], ctx_a[:, k, :], ACT.Copy).then_inc(ctx_hi_done, 1)

            def square(n, b, t, rows, ready, squared):
                act.wait_ge(ready, TT * b + t + 1)
                wait_past(act, squared, TT * b + t)
                nc.scalar.activation(squares[n][:, :], rows[:, t, :], ACT.Square,
                                     accum_out=sum_sq[n][:, t:t + 1]).then_inc(squared, 1)

            def x1T_high(b, k):
                act.wait_ge(x1_transposed, KT * b + k + 1)
                wait_past(act, up_ready, JT * b)
                nc.scalar.activation(x1T_hi[:, k, :], ps_x[k][:, :], ACT.Copy).then_inc(x1T_hi_done, 1)

            def batch(b, first=False, last=False):
                for j in range(JT):
                    act.wait_ge(up_ready, JT * b + j + 1)
                    wait_past(act, h_lo_done, JT * b + j + 1 - BUFS)
                    nc.scalar.activation(hidden[:, j % BUFS, :], ps_h[j % BUFS][:, :], ACT.Silu,
                                         bias=b1_c[:, j:j + 1]).then_inc(hidden_ready, 1)
                    if first and j in CHUNK_AT:
                        split_chunk(CHUNK_AT[j])
                    if not last and j in CTX_AT:
                        context_high(b + 1, CTX_AT[j])
                    if not last and j - 1 in WO_AT:
                        square(0, b + 1, WO_AT[j - 1], x1, resid1_ready, squared1)
                if not last:
                    square(0, b + 1, TT - 1, x1, resid1_ready, squared1)
                for t in range(TT):
                    square(1, b, t, y, resid2_ready, squared2)
                    if t == 1 and not last:
                        for k in range(KT):
                            x1T_high(b + 1, k)

            for k in range(KT):
                context_high(0, k)
            split_chunk(0)
            for t in range(TT):
                square(0, 0, t, x1, resid1_ready, squared1)
            split_chunk(1)
            split_chunk(2)
            for k in range(KT):
                x1T_high(0, k)
            act.wait_ge(consts_loaded, 4 * DMA)
            act.wait_ge(chunk_lo, W1_CHUNKS)
            batch(0, first=True)
            with act.Fori(1, LAST) as b:
                batch(b)
            batch(LAST, last=True)

        @block.vector
        def _(dve):
            def split_chunk(i):
                buf, _, hi, lo = CHUNKS[i]
                dve.wait_ge(chunk_hi, i + 1)
                nc.vector.tensor_tensor(lo, buf, hi.bitcast(FP32), ALU.subtract).then_inc(chunk_lo, 1)

            def context_low(b, k):
                dve.wait_ge(ctx_hi_done, KT * b + k + 1)
                nc.vector.tensor_tensor(ctx_lo[:, k, :], ctx_a[:, k, :], ctx_hi[:, k, :].bitcast(FP32),
                                        ALU.subtract).then_inc(ctx_split, 1)

            def first_residual(b, t):
                dve.wait_ge(wo_ready, TT * b + t + 1)
                dve.wait_ge(xbo_ready, TT * b + t + 1)
                nc.vector.tensor_tensor(x1[:, t, :], ps_x[t % 2][:, 0:D], x1[:, t, :], ALU.add)\
                    .then_inc(resid1_ready, 1)

            def first_scale(b, t):
                dve.wait_ge(rms1_ready, TT * b + t + 1)
                nc.vector.scalar_tensor_tensor(out=x1[:, t, :], in0=x1[:, t, :], scalar=rms[0][:, t:t + 1],
                                               in1=alpha1_b[:, :], op0=ALU.mult, op1=ALU.mult)\
                    .then_inc(scaled1, 1)

            def x1T_low(b, k):
                dve.wait_ge(x1T_hi_done, KT * b + k + 1)
                nc.vector.tensor_tensor(x1T_lo[:, k, :], ps_x[k][:, :], x1T_hi[:, k, :].bitcast(FP32),
                                        ALU.subtract).then_inc(x1T_lo_done, 1)

            def second_residual(b, t):
                dve.wait_ge(down_ready, TT * b + t + 1)
                dve.wait_ge(xb2_ready, TT * b + t + 1)
                nc.vector.tensor_tensor(y[:, t, :], ps_y[t % 2][:, 0:D], y[:, t, :], ALU.add)\
                    .then_inc(resid2_ready, 1)

            def second_norm(b, t):
                dve.wait_ge(rms2_ready, TT * b + t + 1)
                nc.vector.scalar_tensor_tensor(out=y[:, t, :], in0=y[:, t, :], scalar=rms[1][:, t:t + 1],
                                               in1=alpha2_b[:, :], op0=ALU.mult, op1=ALU.mult)\
                    .then_inc(scaled2, 1)
                dve.wait_ge(xg_ready, TT * b + t + 1)
                dve.wait_ge(scaled2, TT * b + t + 1)
                nc.vector.tensor_tensor(z[:, t, :], y[:, t, :], z[:, t, :], ALU.add).then_inc(summed, 1)
                dve.wait_ge(summed, TT * b + t + 1)
                nc.vector.bn_stats(stats[:, t, :], z[:, t, :]).then_inc(stats_done, 1)
                wait_apart(dve, stats_done, TT * b + t + 1, consts_loaded)
                nc.vector.bn_aggr(mean_var[:, t, :], stats[:, t, :]).then_inc(aggregated, 1)

            def finish(b, t):
                dve.wait_ge(inv_std_ready, TT * b + t + 1)
                nc.vector.tensor_scalar(z[:, t, :], z[:, t, :], mean_var[:, t, 0:1], inv_std[:, t:t + 1],
                                        ALU.subtract, ALU.mult).then_inc(out_ready, 1)

            def batch(b, first=False, last=False):
                for j in range(JT):
                    if j == 0:
                        wait_past(dve, down_ready, TT * b)
                    dve.wait_ge(hidden_ready, JT * b + j + 1)
                    nc.vector.tensor_copy(h_hi[:, j, :], hidden[:, j % BUFS, :]).then_inc(h_hi_done, 1)
                    dve.wait_ge(h_hi_done, JT * b + j + 1)
                    nc.vector.tensor_tensor(h_lo[:, j, :], hidden[:, j % BUFS, :], h_hi[:, j, :].bitcast(FP32),
                                            ALU.subtract).then_inc(h_lo_done, 1)
                    if first and j in CHUNK_AT:
                        split_chunk(CHUNK_AT[j])
                    if j == 1 and not first:
                        second_norm(b - 1, TT - 1)
                        finish(b - 1, TT - 2)
                    if j == 3 and not first:
                        finish(b - 1, TT - 1)
                    if not last and j in CTX_AT:
                        context_low(b + 1, CTX_AT[j])
                    if not last and j - 1 in WO_AT:
                        first_residual(b + 1, WO_AT[j - 1])
                        if WO_AT[j - 1] > 0:
                            first_scale(b + 1, WO_AT[j - 1] - 1)
                if not last:
                    first_residual(b + 1, TT - 1)
                    first_scale(b + 1, TT - 2)
                    first_scale(b + 1, TT - 1)
                for t in range(TT):
                    second_residual(b, t)
                    if t >= 1:
                        second_norm(b, t - 1)
                    if t >= 2:
                        finish(b, t - 2)
                    if t == 1 and not last:
                        for k in range(KT):
                            x1T_low(b + 1, k)

            for k in range(KT):
                context_low(0, k)
            split_chunk(0)
            dve.wait_ge(first_consts_loaded, 3 * DMA)
            for t in range(TT):
                first_residual(0, t)
                if t > 0:
                    first_scale(0, t - 1)
            first_scale(0, TT - 1)
            split_chunk(1)
            split_chunk(2)
            for k in range(KT):
                x1T_low(0, k)
            dve.wait_ge(consts_loaded, 4 * DMA)
            batch(0, first=True)
            with dve.Fori(1, LAST) as b:
                batch(b)
            batch(LAST, last=True)
            second_norm(LAST, TT - 1)
            finish(LAST, TT - 2)
            finish(LAST, TT - 1)

        @block.tensor
        def _(pe):
            def three_passes(out_ps, pairs, done):
                n = 0
                for (a_hi, a_lo), (b_hi, b_lo) in pairs:
                    for lhsT, rhs in ((a_hi, b_hi), (a_hi, b_lo), (a_lo, b_hi)):
                        last = nc.tensor.matmul(out_ps, lhsT=lhsT, rhs=rhs, start=(n == 0),
                                                stop=(n == 3 * len(pairs) - 1))
                        n += 1
                last.then_inc(done, 1)

            def project_out(b, t):
                if t < 2:
                    wait_past(pe, x1T_lo_done, KT * b)
                else:
                    pe.wait_ge(resid1_ready, TT * b + t - 1)
                toks = slice(t * P, (t + 1) * P)
                three_passes(ps_x[t % 2][:, 0:D],
                             [((ctx_hi[:, k, toks], ctx_lo[:, k, toks]), (wo_hi[:, k, :], wo_lo[:, k, :]))
                              for k in range(KT)], wo_ready)

            def transpose_x1(b):
                pe.wait_ge(x1_ready, TT * (b + 1))
                pe.wait_ge(resid1_ready, TT * (b + 1))
                for k in range(KT):
                    for t in range(TT):
                        last = nc.tensor.transpose(ps_x[k][:, t * P:(t + 1) * P], x1[:, t, k * P:(k + 1) * P],
                                                   ident[:, :])
                    last.then_inc(x1_transposed, 1)

            def batch(b, first=False, last=False):
                pe.wait_ge(x1T_lo_done, KT * (b + 1))
                for j in range(JT):
                    wait_past(pe, hidden_ready, JT * b + j + 1 - BUFS)
                    cols = slice(j * P, (j + 1) * P)
                    three_passes(ps_h[j % BUFS][:, :],
                                 [((w1_hi[:, k, cols], w1_lo[:, k, cols]), (x1T_hi[:, k, :], x1T_lo[:, k, :]))
                                  for k in range(KT)], up_ready)
                    if not last and j in WO_AT:
                        if WO_AT[j] == 0:
                            pe.wait_ge(ctx_split, KT * (b + 2))
                        project_out(b + 1, WO_AT[j])
                if first:
                    pe.wait_ge(chunk_lo, len(CHUNKS))
                for t in range(TT):
                    wait_past(pe, resid2_ready, TT * b + t + 1 - 2)
                    toks = slice(t * P, (t + 1) * P)
                    n = 0
                    for j in range(JT):
                        if t == 0:
                            pe.wait_ge(h_lo_done, JT * b + j + 1)
                        for lhsT, rhs in ((h_hi[:, j, toks], w2_hi[:, j, :]), (h_hi[:, j, toks], w2_lo[:, j, :]),
                                          (h_lo[:, j, toks], w2_hi[:, j, :])):
                            end = nc.tensor.matmul(ps_y[t % 2][:, 0:D], lhsT=lhsT, rhs=rhs, start=(n == 0),
                                                   stop=(n == 3 * JT - 1))
                            n += 1
                    end.then_inc(down_ready, 1)
                    if t == 1 and not last:
                        transpose_x1(b + 1)

            pe.wait_ge(consts_ready, 3)
            pe.wait_ge(ctx_split, KT)
            for t in range(TT):
                project_out(0, t)
            transpose_x1(0)
            pe.wait_ge(chunk_lo, W1_CHUNKS)
            batch(0, first=True)
            with pe.Fori(1, LAST) as b:
                batch(b)
            batch(LAST, last=True)


def transformer_layer(nc, x, xT, adj, wq, bqT, wk, bkT, wv, bv, wo, bo, w1, b1T, w2, b2,
                      alpha1, gamma1, alpha2, gamma2, out):
    ctx_dram = nc.dram_tensor("ctx_dram", (B, 2, D, N), FP32, kind="Internal").ap()
    with ExitStack() as stack:
        shared = Shared(nc, stack)
        attention_phase(nc, shared, xT, adj, wq, bqT, wk, bkT, wv, bv, wo, ctx_dram)
        feed_forward_phase(nc, shared, x, ctx_dram, bo, w1, b1T, w2, b2, alpha1, gamma1, alpha2, gamma2, out)


def kernel(x, adj, **layer):
    import numpy as _np
    import concourse.bacc as _bacc
    from concourse.bass_utils import run_bass_kernel_spmd as _run

    w = {name.removeprefix("L0_gnn_"): _np.asarray(a) for name, a in layer.items()}
    x = _np.asarray(x)

    def per_partition(v, tiles):
        return v.reshape(tiles, -1).T

    ins = [("x", x), ("xT", x.transpose(0, 2, 1)), ("adj", _np.asarray(adj)),
           ("wq", w["wq"]), ("bqT", per_partition(w["bq"], KT)),
           ("wk", w["wk"]), ("bkT", per_partition(w["bk"], KT)),
           ("wv", w["wv"]), ("bv", per_partition(w["bv"], H)),
           ("wo", w["wo"]), ("bo", w["bo"]), ("w1", w["w1"]), ("b1T", per_partition(w["b1"], JT)),
           ("w2", w["w2"]), ("b2", w["b2"]), ("alpha1", w["alpha1"]), ("gamma1", w["gamma1"]),
           ("alpha2", w["alpha2"]), ("gamma2", w["gamma2"])]
    nc = _bacc.Bacc("TRN2", target_bir_lowering=False, num_devices=1)
    arrays, args = {}, []
    for name, a in ins:
        arrays[f"in_{name}"] = _np.ascontiguousarray(a)
        args.append(nc.dram_tensor(f"in_{name}", a.shape, mybir.dt.from_np(a.dtype), kind="ExternalInput").ap())
    args.append(nc.dram_tensor("out_0", (B, N, D), FP32, kind="ExternalOutput").ap())
    transformer_layer(nc, *args)
    r = _run(nc, [arrays], core_ids=[0])
    return r.results[0]["out_0"]
```
